# Optimizing a Trainium2 kernel written in Bass

```python
import numpy as np
import jax
import jax.numpy as jnp

def _softmax(x, axis=-1):
    return jax.nn.softmax(x, axis=axis)

def _gelu(x):
    return jax.nn.gelu(x, approximate=True)

def _silu(x):
    return jax.nn.silu(x)

def _sigmoid(x):
    return jax.nn.sigmoid(x)

def _layernorm(x, axis=-1, eps=1e-05):
    m = jnp.mean(x, axis=axis, keepdims=True)
    v = jnp.var(x, axis=axis, keepdims=True)
    return (x - m) / jnp.sqrt(v + eps)

def _scatter_add(tgt, idx, src, axis=0):
    return tgt.at[idx].add(src)

def _segment_sum(src, seg, n):
    return jax.ops.segment_sum(src, seg, n)
kernel_name = 'mk_adj_preln_d1_adj_r2_279961'

def setup_inputs(seed: int=0):
    np.random.seed(seed)
    _w = jnp.asarray

    def _rec_inputs():
        import jax
        import jax.numpy as jnp
        _gk = jax.random.key(seed)
        x = -9.806e-05 + 1 * jax.random.normal(jax.random.fold_in(_gk, 1), (8192, 64), jnp.float32)
        _w = (1.0 + jnp.arange(8192, dtype=jnp.float32)) ** (-0.5)
        _w = _w / _w.mean()
        _pij = jnp.clip(0.000244141 * _w[:, None] * _w[None, :], 0.0, 1.0)
        _a = jax.random.uniform(jax.random.fold_in(_gk, 2), (8192, 8192)) < _pij
        adj = _a.astype(jnp.int32)
        return (x, adj)
    x, adj = _rec_inputs()

    def _L0_gnn_setup():
        import jax, jax.numpy as jnp
        import numpy as np
        ALPHA = 0.2
        MASK_VAL = -9000000000000000.0
        key = jax.random.key(seed)
        k1, k2, k3 = jax.random.split(key, 3)
        N, D = (4096, 64)
        h = jax.random.normal(k1, (N, D), dtype=jnp.float32)
        adj = jax.random.randint(k2, (N, N), 0, 2, dtype=jnp.int32)
        a = jax.random.normal(k3, (2 * D, 1), dtype=jnp.float32) * (1.414 / np.sqrt(D))
        return {'h': h, 'adj': adj, 'a': a}
    _L0_gnn_all = _L0_gnn_setup()
    _L0_gnn_in = {k: v for k, v in _L0_gnn_all.items() if k in ('a',)}
    del _L0_gnn_all
    return {'x': x, 'adj': adj, 'L0_gnn_a': _L0_gnn_in['a']}

def reference(x, adj, L0_gnn_a):
    import jax
    import jax.numpy as jnp

    def _L0_gnn_ref(h, adj, a):
        import jax, jax.numpy as jnp
        import numpy as np
        ALPHA = 0.2
        MASK_VAL = -9000000000000000.0
        D = h.shape[1]
        wh1 = h @ a[:D, :]
        wh2 = h @ a[D:, :]
        e = wh1 + wh2.T
        e = jnp.where(e > 0, e, ALPHA * e)
        scores = jnp.where(adj > 0, e, MASK_VAL)
        attention = jax.nn.softmax(scores, axis=1)
        h_prime = attention @ h
        return jax.nn.relu(h_prime)
    h = jnp.maximum(_layernorm(x, axis=-1), 0.0)
    x = x + _L0_gnn_ref(h, adj, L0_gnn_a)
    return x

_drawn_inputs = setup_inputs


def setup_inputs(seed=0):
    import zlib

    import numpy as np

    out = dict(_drawn_inputs(seed))
    spreads = {}
    factors = {}
    for name, (base, spread) in spreads.items():
        noise = np.random.default_rng([zlib.crc32(name.encode()), seed]).standard_normal(out[name].shape)
        drawn = base * np.exp(spread * noise) if base else spread * noise
        out[name] = jnp.asarray(drawn.astype(out[name].dtype))
    for name, factor in factors.items():
        out[name] = (out[name] * factor).astype(out[name].dtype)
    return out
```

```python
from contextlib import ExitStack

import concourse.bass as bass
from concourse import mybir

ALU = mybir.AluOpType
ACT = mybir.ActivationFunctionType
AX = mybir.AxisListType
F32 = mybir.dt.float32
BF16 = mybir.dt.bfloat16
F16 = mybir.dt.float16
I32 = mybir.dt.int32
RMAX = bass.bass_isa.ReduceOp.max
RADD = bass.bass_isa.ReduceOp.add

P = 128
LEAK = 0.2
EPS = 1e-5
BIG = 2.0 ** 64
LOW = 2.0 ** 11
SCALE = 2.0 ** 12
EDGE = 2000.0

TILES = 4
ROWS = TILES * P
SLOT_CHUNKS = 4
SLOTS = 4
PAIR = 2
TURN_RING = 2
RING = 4


def gat_layer(nc, x, adj, a, out):
    N, D = x.shape
    NC = N // P
    NB = N // ROWS
    W = D + 1
    BODY = SLOT_CHUNKS * SLOTS
    ITERS = NC // BODY
    PAIRS = BODY // PAIR
    SLOT_PAIRS = SLOT_CHUNKS // PAIR
    SLOT_COLS = SLOT_CHUNKS * P
    assert NC % BODY == 0 and N % ROWS == 0 and PAIRS % RING == 0

    x_cols = x.rearrange("(c p) d -> p c d", p=P)
    out_rows = out.rearrange("(b t p) d -> p b t d", p=P, t=TILES)
    adj_rows = adj.rearrange("(b t p) j -> p b t j", p=P, t=TILES)
    a_row = a.rearrange("k o -> o k")
    s_dram = nc.dram_tensor("s_dram", (NC, P), F32, kind="Internal").ap()
    s_flat = s_dram.rearrange("(o c) p -> o (c p)", o=1)

    with ExitStack() as ctx:
        def sb(name, shape, dt=F32):
            return ctx.enter_context(nc.sbuf_tensor(name, [P] + shape, dt))

        def sem(name):
            return ctx.enter_context(nc.semaphore(name))

        turned = ctx.enter_context(nc.psum_tensor("turned", [P, TURN_RING, PAIR, ROWS], F32))
        acc = ctx.enter_context(nc.psum_tensor("acc", [P, TILES, 512], F32))

        xt = sb("xt", [NC, D])
        ident = sb("ident", [P])
        s_row = sb("s_row", [N])
        t = sb("t", [NC])
        neg_t = sb("neg_t", [NC])
        t_big = sb("t_big", [NC])
        val1 = sb("val1", [NC, 2 * W], F16)
        val2 = sb("val2", [NC, 2 * W], F16)
        coef = sb("coef", [NC, 4])
        h_sum = sb("h_sum", [D])
        zero_w = sb("zero_w", [P], BF16)
        zero_v = sb("zero_v", [4 * W], BF16)
        edge_bias = sb("edge_bias", [1])
        edges = sb("edges", [SLOTS, TILES, SLOT_COLS], I32)
        mask = sb("mask", [RING, PAIR, ROWS], BF16)
        side = sb("side", [RING, PAIR, ROWS], BF16)
        split = sb("split", [2, RING, PAIR, ROWS], BF16)
        pos, neg = split[:, 0], split[:, 1]
        sums = sb("sums", [TILES, 4, W])
        scaled = sb("scaled", [TILES, 4, W])
        comb = sb("comb", [TILES, 2, W])
        total = sb("total", [TILES, W])
        lone = sb("lone", [TILES])
        fill = sb("fill", [TILES, D])
        filled = sb("filled", [TILES, D])
        den = sb("den", [TILES])
        inv = sb("inv", [TILES])
        att = sb("att", [TILES, D])
        y = sb("y", [TILES, D])
        h = sb("h", [NC, D])
        big = sb("big", [NC, W])
        work = big[:].rearrange("p c w -> p (c w)")[:, 0:NC * D].rearrange("p (c d) -> p c d", d=D)
        work2 = split[:].rearrange("p m r c i -> p (m r c i)").bitcast(F32).rearrange("p (c d) -> p c d", d=D)
        a_b = sb("a_b", [2 * D])
        mean = sb("mean", [NC])
        var = sb("var", [NC])
        std = sb("std", [NC])
        quo = sb("quo", [NC])
        rstd = sb("rstd", [NC])
        s = sb("s", [NC])
        s_t = sb("s_t", [P])
        ext = sb("ext", [2])
        ext_all = sb("ext_all", [2])
        eb = sb("eb", [2])
        bexp = sb("bexp", [NC])
        dexp = sb("dexp", [NC])
        xs = sb("xs", [NC])
        xm = sb("xm", [NC])
        x1 = sb("x1", [NC])
        x2 = sb("x2", [NC])
        e1 = sb("e1", [NC])
        e2 = sb("e2", [NC])
        hp = sb("hp", [D])

        x_in = sem("x_in")
        a_in = sem("a_in")
        ident_set = sem("ident_set")
        ident_zero = sem("ident_zero")
        consts_set = sem("consts_set")
        centred = sem("centred")
        squared = sem("squared")
        var_ready = sem("var_ready")
        std_ready = sem("std_ready")
        h_ready = sem("h_ready")
        hs_ready = sem("hs_ready")
        s_ready = sem("s_ready")
        s_turned = sem("s_turned")
        s_rows = sem("s_rows")
        s_out = sem("s_out")
        s_in = sem("s_in")
        ext_ready = sem("ext_ready")
        ext_all_ready = sem("ext_all_ready")
        exp_bias = sem("exp_bias")
        exp_ready = sem("exp_ready")
        row_args = sem("row_args")
        row_exp = sem("row_exp")
        hp_ready = sem("hp_ready")
        h_sum_ready = sem("h_sum_ready")
        values_ready = sem("values_ready")
        coef_ready = sem("coef_ready")
        dve_seq = sem("dve_seq")

        slot_in = [sem(f"slot_in{i}") for i in range(SLOTS)]
        turn_done = sem("turn_done")
        mask_done = sem("mask_done")
        side_act = sem("side_act")
        side_dve = sem("side_dve")
        split_done = sem("split_done")
        used = sem("used")
        tile_done = sem("tile_done")
        drained = sem("drained")
        pool_seq = sem("pool_seq")
        combined = sem("combined")
        inv_done = sem("inv_done")
        att_done = sem("att_done")
        y_done = sem("y_done")
        y_out = sem("y_out")

        block = ctx.enter_context(nc.Block())

        @block.sync
        def _(sp):
            def load(slot, b, it):
                col = it * (BODY * P) + slot * SLOT_COLS
                sp.dma_start(edges[:, slot], adj_rows[:, b, :, bass.ds(col, SLOT_COLS)]).then_inc(slot_in[slot], 16)

            def body(b, it):
                for slot in range(SLOTS):
                    sp.wait_ge(turn_done, ((b * ITERS + it - 1) * SLOTS + slot + 1) * SLOT_PAIRS)
                    load(slot, b, it)

            def store(b):
                sp.wait_ge(y_done, b + 1)
                sp.dma_start(out_rows[:, b], y[:]).then_inc(y_out, 16)

            sp.dma_start(xt[:], x_cols).then_inc(x_in, 16)
            sp.dma_start(a_b[:], a_row.to_broadcast([P, 2 * D])).then_inc(a_in, 16)
            for slot in range(SLOTS):
                load(slot, 0, 0)
            sp.wait_ge(s_rows, 1)
            sp.dma_start(s_dram, s_t[0:NC, :]).then_inc(s_out, 16)
            sp.wait_ge(s_out, 16)
            sp.dma_start(s_row[:], s_flat.to_broadcast([P, N])).then_inc(s_in, 16)
            with sp.Fori(1, ITERS) as it:
                body(0, it)
            with sp.Fori(1, NB) as b:
                with sp.Fori(0, ITERS) as it:
                    body(b, it)
                store(b - 1)
            store(NB - 1)
            sp.wait_ge(y_out, 16 * NB)

        @block.gpsimd
        def _(pool):
            pool.memset(ident[:], 0.0).then_inc(ident_zero, 1)
            pool.wait_ge(ident_zero, 1)
            pool.affine_select(out=ident[:], in_=ident[:], compare_op=ALU.not_equal, fill=1.0, base=0,
                               pattern=[[-1, P]], channel_multiplier=1).then_inc(ident_set, 1)
            pool.wait_ge(h_ready, 1)
            pool.wait_ge(a_in, 16)
            pool.tensor_tensor(work2, h[:], a_b[:, 0:D].unsqueeze(1).to_broadcast([P, NC, D]),
                               ALU.mult).then_inc(hs_ready, 1)
            pool.wait_ge(ext_ready, 2)
            pool.partition_all_reduce(ext_all[:], ext[:], P, RMAX).then_inc(ext_all_ready, 1)
            pool.wait_ge(hp_ready, 1)
            pool.partition_all_reduce(h_sum[:], hp[:], P, RADD).then_inc(h_sum_ready, 1)
            pool.wait_ge(h_sum_ready, 1)
            pool.wait_ge(coef_ready, 4)

            def combine(b):
                seq = b * 4
                cf = coef[:, bass.ds(b * TILES, TILES), :].unsqueeze(3).to_broadcast([P, TILES, 4, W])
                pool.wait_ge(drained, (b + 2) * TILES)
                pool.tensor_tensor(scaled[:], sums[:], cf, ALU.mult).then_inc(pool_seq, 1)
                pool.wait_ge(pool_seq, seq + 1)
                pool.tensor_tensor(comb[:], scaled[:, :, 0:2], scaled[:, :, 2:4], ALU.add).then_inc(pool_seq, 1)
                pool.wait_ge(pool_seq, seq + 2)
                pool.tensor_tensor(total[:], comb[:, :, 0], comb[:, :, 1], ALU.add).then_inc(combined, 1)
                pool.wait_ge(inv_done, (b + 1) * 3)
                pool.tensor_tensor(fill[:], h_sum[:].unsqueeze(1).to_broadcast([P, TILES, D]),
                                   lone[:].unsqueeze(2).to_broadcast([P, TILES, D]), ALU.mult).then_inc(pool_seq, 1)
                pool.wait_ge(pool_seq, seq + 3)
                pool.tensor_tensor(filled[:], total[:, :, 0:D], fill[:], ALU.add).then_inc(pool_seq, 1)
                pool.wait_ge(pool_seq, seq + 4)
                if first_done:
                    pool.wait_ge(y_done, b)
                pool.tensor_tensor(att[:], filled[:], inv[:].unsqueeze(2).to_broadcast([P, TILES, D]),
                                   ALU.mult).then_inc(att_done, 1)

            first_done = False
            combine(0)
            first_done = True
            with pool.Fori(1, NB) as b:
                combine(b)

        @block.scalar
        def _(act):
            act.wait_ge(centred, 1)
            act.activation(work, h[:], ACT.Square).then_inc(squared, 1)
            act.wait_ge(var_ready, 1)
            act.activation(std[:], var[:], ACT.Sqrt).then_inc(std_ready, 1)
            act.wait_ge(exp_bias, 2)
            act.activation(bexp[:], t[:], ACT.Exp, bias=eb[:, 0:1], scale=1.0).then_inc(exp_ready, 1)
            act.activation(dexp[:], t[:], ACT.Exp, bias=eb[:, 1:2], scale=LEAK).then_inc(exp_ready, 1)
            act.wait_ge(row_args, 2)
            act.activation(e1[:], x1[:], ACT.Exp).then_inc(row_exp, 1)
            act.activation(e2[:], x2[:], ACT.Exp).then_inc(row_exp, 1)
            act.sem_inc(drained, TILES)
            act.wait_ge(consts_set, 4)
            act.wait_ge(s_in, 16)

            def body(b, it, first=False, drain_at=None):
                for g in range(PAIRS):
                    q, r = (b * ITERS + it) * PAIRS + g, g % RING
                    act.wait_ge(turn_done, q + 1)
                    if not first or g >= RING:
                        act.wait_ge(split_done, q - RING + 1)
                    act.activation(mask[:, r], turned[:, g % TURN_RING].bitcast(I32), ACT.Sigmoid,
                                   bias=edge_bias[:, 0:1], scale=EDGE).then_inc(mask_done, 1)
                    act.activation(side[:, r, 0], s_row[:, bass.ds(b * ROWS, ROWS)], ACT.Relu,
                                   bias=t_big[:, bass.ds(it * BODY + g * PAIR, 1)], scale=BIG).then_inc(side_act, 1)
                    if g == drain_at:
                        drain(b - 1)

            def drain(b):
                for k in range(TILES):
                    if k < TILES - 1:
                        act.wait_ge(tile_done, b * (TILES - 1) + k + 1)
                    else:
                        act.wait_ge(used, (b + 1) * ITERS * PAIRS)
                    act.activation(sums[:, k], acc[:, k, 0:4 * W].rearrange("p (k w) -> p k w", w=W),
                                   ACT.Copy).then_inc(drained, 1)

            body(0, 0, first=True)
            with act.Fori(1, ITERS) as it:
                body(0, it)
            body(1, 0, drain_at=1)
            with act.Fori(1, ITERS) as it:
                body(1, it)
            with act.Fori(2, NB) as b:
                act.wait_ge(y_done, b - 1)
                body(b, 0, drain_at=1)
                with act.Fori(1, ITERS) as it:
                    body(b, it)
            act.wait_ge(y_done, NB - 1)
            drain(NB - 1)

        @block.tensor
        def _(pe):
            pe.wait_ge(s_ready, 1)
            pe.wait_ge(ident_set, 1)
            pe.transpose(acc[0:NC, 0, 0:P], s[:], ident[:]).then_inc(s_turned, 1)

            def turn(b, it, g):
                if g % SLOT_PAIRS == 0:
                    pe.wait_ge(slot_in[g // SLOT_PAIRS], (b * ITERS + it + 1) * 16)
                for c in range(PAIR):
                    col = (g % SLOT_PAIRS * PAIR + c) * P
                    for k in range(TILES):
                        last = pe.transpose(turned[:, g % TURN_RING, c, k * P:(k + 1) * P],
                                            edges[:, g // SLOT_PAIRS, k, col:col + P].bitcast(F32), ident[:])
                last.then_inc(turn_done, 1)

            def add(b, it, g, last_pair):
                q, r = (b * ITERS + it) * PAIRS + g, g % RING
                pe.wait_ge(split_done, q + 1)
                for k in range(TILES):
                    for c in range(PAIR):
                        chunk = it * BODY + g * PAIR + c
                        for m, val, o in ((pos, val1, 0), (neg, val2, 2 * W)):
                            mm = pe.matmul(acc[:, k, o:o + 2 * W], m[:, r, c, k * P:(k + 1) * P],
                                           val[:, bass.ds(chunk, 1), :].squeeze(1), start=False,
                                           stop=last_pair and c == PAIR - 1, skip_group_check=True)
                    if last_pair and k < TILES - 1:
                        mm.then_inc(tile_done, 1)
                mm.then_inc(used, 1)

            def body(b, it, ahead, first=False, last=False):
                for g in range(PAIRS):
                    q = (b * ITERS + it) * PAIRS + g
                    if g + TURN_RING < PAIRS or ahead:
                        pe.wait_ge(mask_done, q + 1)
                        if g + TURN_RING < PAIRS:
                            turn(b, it, g + TURN_RING)
                        else:
                            turn(*ahead, g + TURN_RING - PAIRS)
                    if first and g == 0:
                        for k in range(TILES):
                            pe.wait_ge(drained, b * TILES + k + 1)
                            pe.matmul(acc[:, k, 0:4 * W], zero_w[:], zero_v[:], start=True, stop=False,
                                      skip_group_check=True)
                    add(b, it, g, last and g == PAIRS - 1)

            def rows(b, ahead):
                body(b, 0, (b, 1), first=True)
                with pe.Fori(1, ITERS - 1) as it:
                    body(b, it, (b, it + 1))
                body(b, ITERS - 1, ahead, last=True)

            pe.wait_ge(s_rows, 1)
            for g in range(TURN_RING):
                turn(0, 0, g)
            pe.wait_ge(consts_set, 4)
            pe.wait_ge(values_ready, 4)
            with pe.Fori(0, NB - 1) as b:
                rows(b, (b + 1, 0))
            rows(NB - 1, None)

        @block.vector
        def _(v):
            steps = [0]

            def link(ins):
                steps[0] += 1
                ins.then_inc(dve_seq, 1)
                v.wait_ge(dve_seq, steps[0])

            def per_chunk(ap, n=D):
                return ap.unsqueeze(2).to_broadcast([P, NC, n])

            v.memset(zero_w[:], 0.0).then_inc(consts_set, 1)
            v.memset(zero_v[:], 0.0).then_inc(consts_set, 1)
            v.memset(edge_bias[:], -EDGE / 2).then_inc(consts_set, 1)
            v.wait_ge(x_in, 16)
            link(v.tensor_reduce(mean[:], xt[:], AX.X, ALU.add))
            link(v.tensor_scalar(mean[:], mean[:], 1.0 / D, None, ALU.mult))
            v.tensor_tensor(h[:], xt[:], per_chunk(mean[:]), ALU.subtract).then_inc(centred, 1)
            v.wait_ge(squared, 1)
            link(v.tensor_reduce(var[:], work, AX.X, ALU.add))
            v.tensor_scalar(var[:], var[:], 1.0 / D, EPS, ALU.mult, ALU.add).then_inc(var_ready, 1)
            v.wait_ge(std_ready, 1)
            link(v.reciprocal(quo[:], std[:]))
            link(v.tensor_tensor(quo[:], quo[:], var[:], ALU.mult))
            link(v.tensor_tensor(quo[:], quo[:], std[:], ALU.add))
            link(v.tensor_scalar(quo[:], quo[:], 0.5, None, ALU.mult))
            link(v.reciprocal(rstd[:], quo[:]))
            v.wait_ge(centred, 1)
            v.scalar_tensor_tensor(out=h[:], in0=h[:], scalar=0.0, in1=per_chunk(rstd[:]), op0=ALU.max,
                                   op1=ALU.mult).then_inc(h_ready, 1)
            v.wait_ge(h_ready, 1)
            v.wait_ge(a_in, 16)
            link(v.tensor_tensor(work, h[:], a_b[:, D:2 * D].unsqueeze(1).to_broadcast([P, NC, D]), ALU.mult))
            link(v.tensor_reduce(t[:], work, AX.X, ALU.add))
            v.tensor_scalar(t_big[:], t[:], BIG, None, ALU.mult).then_inc(consts_set, 1)
            v.wait_ge(hs_ready, 1)
            v.tensor_reduce(s[:], work2, AX.X, ALU.add).then_inc(s_ready, 1)
            v.tensor_reduce(ext[:, 0:1], t[:], AX.X, ALU.max).then_inc(ext_ready, 1)
            link(v.tensor_scalar(neg_t[:], t[:], -1.0, None, ALU.mult))
            v.tensor_reduce(ext[:, 1:2], neg_t[:], AX.X, ALU.max).then_inc(ext_ready, 1)
            v.wait_ge(s_turned, 1)
            v.tensor_copy(s_t[0:NC, :], acc[0:NC, 0, 0:P]).then_inc(s_rows, 1)
            v.tensor_reduce(hp[:], h[:].rearrange("p c d -> p d c"), AX.X, ALU.add).then_inc(hp_ready, 1)
            v.wait_ge(ext_all_ready, 1)
            v.tensor_scalar(eb[:, 0:1], ext_all[:, 0:1], -1.0, None, ALU.mult).then_inc(exp_bias, 1)
            v.tensor_scalar(eb[:, 1:2], ext_all[:, 0:1], -LEAK, None, ALU.mult).then_inc(exp_bias, 1)
            v.wait_ge(s_ready, 1)
            link(v.tensor_scalar(xs[:], s[:], ext_all[:, 0:1], None, ALU.add))
            link(v.scalar_tensor_tensor(out=xm[:], in0=xs[:], scalar=LEAK, in1=xs[:], op0=ALU.mult, op1=ALU.max))
            v.tensor_tensor(x1[:], xs[:], xm[:], ALU.subtract).then_inc(row_args, 1)
            v.scalar_tensor_tensor(out=x2[:], in0=xs[:], scalar=LEAK, in1=xm[:], op0=ALU.mult,
                                   op1=ALU.subtract).then_inc(row_args, 1)
            v.wait_ge(exp_ready, 2)
            for e, val in ((bexp, val1), (dexp, val2)):
                link(v.tensor_scalar(e[:], e[:], SCALE * LOW, None, ALU.mult))
                link(v.tensor_tensor(big[:, :, 0:D], h[:], per_chunk(e[:]), ALU.mult))
                link(v.tensor_copy(big[:, :, D], e[:]))
                v.tensor_scalar(val[:, :, 0:W], big[:], 1.0 / LOW, None, ALU.mult).then_inc(values_ready, 1)
                v.wait_ge(values_ready, 1 if val is val1 else 3)
                v.scalar_tensor_tensor(out=val[:, :, W:2 * W], in0=val[:, :, 0:W], scalar=-LOW, in1=big[:],
                                       op0=ALU.mult, op1=ALU.add).then_inc(values_ready, 1)
                v.wait_ge(values_ready, 2 if val is val1 else 4)
            v.wait_ge(row_exp, 2)
            for k, e in ((0, e1), (2, e2)):
                v.tensor_copy(coef[:, :, k], e[:]).then_inc(coef_ready, 1)
                v.tensor_scalar(coef[:, :, k + 1], e[:], 1.0 / LOW, None, ALU.mult).then_inc(coef_ready, 1)
            v.wait_ge(s_in, 16)

            def side_half(b, it, g):
                v.tensor_scalar(side[:, g % RING, 1], s_row[:, bass.ds(b * ROWS, ROWS)],
                                neg_t[:, bass.ds(it * BODY + g * PAIR + 1, 1)], BIG, ALU.is_gt,
                                ALU.mult).then_inc(side_dve, 1)

            def body(b, it, first=False, invert_at=None, finish_at=None, static=False):
                side_half(b, it, 0)
                for g in range(PAIRS):
                    q, r = (b * ITERS + it) * PAIRS + g, g % RING
                    if g + 1 < PAIRS:
                        side_half(b, it, g + 1)
                    v.wait_ge(mask_done, q + 1)
                    v.wait_ge(side_act, q + 1)
                    v.wait_ge(side_dve, q + 1)
                    if not first or g >= RING:
                        v.wait_ge(used, q - RING + 1)
                    v.tensor_tensor(pos[:, r], mask[:, r], side[:, r], ALU.min)
                    v.tensor_tensor(neg[:, r], mask[:, r], side[:, r], ALU.is_gt).then_inc(split_done, 1)
                    if g == invert_at:
                        invert(b - 1)
                    if g == finish_at:
                        if not static:
                            v.wait_ge(y_out, 16 * (b - 1))
                        finish(b - 1)

            def invert(b):
                v.wait_ge(combined, b + 1)
                v.tensor_scalar(lone[:], total[:, :, D], 0.0, None, ALU.is_equal).then_inc(inv_done, 1)
                v.wait_ge(inv_done, 3 * b + 1)
                v.scalar_tensor_tensor(out=den[:], in0=lone[:], scalar=float(N), in1=total[:, :, D], op0=ALU.mult,
                                       op1=ALU.add).then_inc(inv_done, 1)
                v.wait_ge(inv_done, 3 * b + 2)
                v.reciprocal(inv[:], den[:]).then_inc(inv_done, 1)

            def finish(b):
                v.wait_ge(att_done, b + 1)
                v.scalar_tensor_tensor(out=y[:], in0=att[:], scalar=0.0, in1=xt[:, bass.ds(b * TILES, TILES), :],
                                       op0=ALU.max, op1=ALU.add).then_inc(y_done, 1)

            body(0, 0, first=True)
            with v.Fori(1, ITERS) as it:
                body(0, it)
            body(1, 0)
            body(1, 1, invert_at=3, finish_at=7, static=True)
            with v.Fori(2, ITERS) as it:
                body(1, it)
            with v.Fori(2, NB) as b:
                body(b, 0)
                body(b, 1, invert_at=3, finish_at=7)
                with v.Fori(2, ITERS) as it:
                    body(b, it)
            invert(NB - 1)
            v.wait_ge(y_out, 16 * (NB - 1))
            finish(NB - 1)
    return nc


def kernel(**inputs):
    import numpy as _np
    import concourse.bacc as _bacc
    from concourse import mybir as _mybir
    from concourse.bass_utils import run_bass_kernel_spmd as _run

    nc = _bacc.Bacc("TRN2", target_bir_lowering=False, num_devices=1)
    arrays, args = {}, []
    for name in ("x", "adj", "L0_gnn_a"):
        v = _np.ascontiguousarray(inputs[name])
        arrays[f"in_{name}"] = v
        args.append(nc.dram_tensor(f"in_{name}", v.shape, _mybir.dt.from_np(v.dtype), kind="ExternalInput").ap())
    out = nc.dram_tensor("out", inputs["x"].shape, _mybir.dt.float32, kind="ExternalOutput").ap()
    gat_layer(nc, *args, out)
    r = _run(nc, [arrays], core_ids=[0])
    return r.results[0]["out"]
```

```python
from contextlib import ExitStack

import concourse.bass as bass
from concourse import mybir

ALU = mybir.AluOpType
ACT = mybir.ActivationFunctionType
AX = mybir.AxisListType
F32 = mybir.dt.float32
BF16 = mybir.dt.bfloat16
F16 = mybir.dt.float16
I16 = mybir.dt.int16
RMAX = bass.bass_isa.ReduceOp.max

P = 128
LEAK = 0.2
EPS = 1e-5
BIG = 2.0 ** 64
LOW = 2.0 ** 11
SCALE = 2.0 ** 12

TILES = 4
ROWS = TILES * P
QUAD = 4
QCOLS = QUAD * P
SLOTS = 8
TURN_RING = 2
SIDE_RING = 4
SPLIT_RING = 4
GROUPS = 4
PART = 16


def gat_layer(nc, x, adj, a, out):
    N, D = x.shape
    NC = N // P
    NB = N // ROWS
    W = D + 1
    BODY = SLOTS * QUAD
    ITERS = NC // BODY
    GC = NC // GROUPS
    GCOLS = GC * P
    assert ITERS * BODY == NC and GCOLS == 2048 and ITERS == 2

    x_cols = x.rearrange("(c p) d -> p c d", p=P)
    out_rows = out.rearrange("(b t p) d -> p b t d", p=P, t=TILES)
    x_rows = x.rearrange("(b t p) d -> p b t d", p=P, t=TILES)
    adj_rows = adj.rearrange("(b t p) j -> p b t j", p=P, t=TILES)
    a_row = a.rearrange("k o -> o k")
    a_cols = a.rearrange("(k d) o -> d (k o)", k=2)

    with ExitStack() as ctx:
        def sb(name, shape, dt=F32):
            return ctx.enter_context(nc.sbuf_tensor(name, [P] + shape, dt))

        def sem(name):
            return ctx.enter_context(nc.semaphore(name))

        turned = ctx.enter_context(nc.psum_tensor("turned", [P, TURN_RING, QUAD * ROWS], BF16))
        acc = ctx.enter_context(nc.psum_tensor("acc", [P, TILES, 512], F32))
        halves = [turned[:].rearrange("p r n -> p (r n)").bitcast(F32), acc[:].rearrange("p t n -> p (t n)")]

        h = sb("h", [NC, D])
        x_block = sb("x_block", [TILES, D])
        ident = sb("ident", [P])
        ident_b = sb("ident_b", [P], BF16)
        s_row = sb("s_row", [N])
        s_block = sb("s_block", [2, ROWS])
        t = sb("t", [NC])
        t_big = sb("t_big", [NC])
        val1 = sb("val1", [NC, 2 * W], F16)
        val2 = sb("val2", [NC, 2 * W], F16)
        coef = sb("coef", [NC, 4])
        h_sum = sb("h_sum", [D])
        zero_w = sb("zero_w", [P], BF16)
        zero_v = sb("zero_v", [4 * W], BF16)
        edges = sb("edges", [SLOTS, TILES, QCOLS], BF16)
        side = sb("side", [SIDE_RING, QUAD * ROWS], BF16)
        split = sb("split", [SPLIT_RING, 2, QUAD * ROWS], BF16)
        sums = sb("sums", [TILES, 4, W])
        comb = sb("comb", [TILES, 2, W])
        total = sb("total", [TILES, W])
        lone = sb("lone", [TILES])
        fill = sb("fill", [TILES, D])
        filled = sb("filled", [TILES, D])
        den = sb("den", [TILES])
        inv = sb("inv", [TILES])
        att = sb("att", [TILES, D])
        y = sb("y", [TILES, D])
        big = sb("big", [2, PART, W])
        prod = side[:].rearrange("p r n -> p (r n)").bitcast(F32).rearrange("p (c d) -> p c d", d=D)
        h_t = split[:].rearrange("p r k n -> p (r k n)").bitcast(F32)
        a_b = sb("a_b", [2 * D])
        a_c = sb("a_c", [2])
        a_rep = sb("a_rep", [P])
        ones = sb("ones", [P])
        mean = sb("mean", [NC])
        var = sb("var", [NC])
        std = sb("std", [NC])
        quo = sb("quo", [NC])
        rstd = sb("rstd", [NC])
        s = sb("s", [NC])
        hs_part = sb("hs_part", [GROUPS])
        hs_col = sb("hs_col", [1])
        hs_diag = sb("hs_diag", [D])
        t_max = sb("t_max", [1])
        top = sb("top", [1])
        eb = sb("eb", [2])
        bexp = sb("bexp", [NC])
        dexp = sb("dexp", [NC])
        xs, xm, x1, x2 = mean, var, std, quo
        e1 = sb("e1", [NC])
        e2 = sb("e2", [NC])

        x_in = [sem(f"x_in{i}") for i in range(2)]
        a_in = sem("a_in")
        ident_zero = sem("ident_zero")
        ident_set = sem("ident_set")
        consts_set = sem("consts_set")
        a_rep_set = sem("a_rep_set")
        centred = sem("centred")
        squared = sem("squared")
        var_ready = sem("var_ready")
        std_ready = sem("std_ready")
        h_ready = sem("h_ready")
        h_turned = sem("h_turned")
        h_t_ready = sem("h_t_ready")
        s_spread = sem("s_spread")
        s_row_ready = sem("s_row_ready")
        t_big_ready = sem("t_big_ready")
        t_max_ready = sem("t_max_ready")
        top_ready = sem("top_ready")
        exp_bias = sem("exp_bias")
        exp_ready = sem("exp_ready")
        big_ready = sem("big_ready")
        near_ready = sem("near_ready")
        values_ready = sem("values_ready")
        diag_ready = sem("diag_ready")
        s_cols = sem("s_cols")
        s_ready = sem("s_ready")
        row_args = sem("row_args")
        row_exp = sem("row_exp")
        coef_ready = sem("coef_ready")
        dve_seq = sem("dve_seq")

        slot_in = [sem(f"slot_in{i}") for i in range(SLOTS)]
        block_ready = sem("block_ready")
        turn_done = sem("turn_done")
        side_done = sem("side_done")
        neg_done = sem("neg_done")
        split_done = sem("split_done")
        used = sem("used")
        tile_done = sem("tile_done")
        drained = sem("drained")
        comb_seq = sem("comb_seq")
        combined = sem("combined")
        inv_done = sem("inv_done")
        x_block_in = sem("x_block_in")
        att_done = sem("att_done")
        y_done = sem("y_done")
        y_out = sem("y_out")

        half = [slice(0, NC // 2), slice(NC // 2, NC)]
        part = [slice(i, i + PART) for i in range(0, NC, PART)]

        def combine(eng, b):
            seq = b * 4
            cf = coef[:, bass.ds(b * TILES, TILES), :].unsqueeze(3).to_broadcast([P, TILES, 4, W])
            eng.wait_ge(drained, (b + 2) * TILES)
            eng.tensor_tensor(sums[:], sums[:], cf, ALU.mult).then_inc(comb_seq, 1)
            eng.wait_ge(comb_seq, seq + 1)
            eng.tensor_tensor(comb[:], sums[:, :, 0:2], sums[:, :, 2:4], ALU.add).then_inc(comb_seq, 1)
            eng.wait_ge(comb_seq, seq + 2)
            eng.tensor_tensor(total[:], comb[:, :, 0], comb[:, :, 1], ALU.add).then_inc(combined, 1)

        def attend(eng, b, first=False):
            seq = b * 4
            eng.wait_ge(inv_done, (b + 1) * 3)
            eng.tensor_tensor(fill[:], h_sum[:].unsqueeze(1).to_broadcast([P, TILES, D]),
                              lone[:].unsqueeze(2).to_broadcast([P, TILES, D]), ALU.mult).then_inc(comb_seq, 1)
            eng.wait_ge(comb_seq, seq + 3)
            eng.tensor_tensor(filled[:], total[:, :, 0:D], fill[:], ALU.add).then_inc(comb_seq, 1)
            eng.wait_ge(comb_seq, seq + 4)
            if not first:
                eng.wait_ge(y_done, b)
            eng.tensor_tensor(att[:], filled[:], inv[:].unsqueeze(2).to_broadcast([P, TILES, D]),
                              ALU.mult).then_inc(att_done, 1)

        block = ctx.enter_context(nc.Block())

        @block.sync
        def _(sp):
            for i in range(2):
                sp.dma_start(h[:, half[i]], x_cols[:, half[i]]).then_inc(x_in[i], 16)
            sp.dma_start(a_b[:], a_row.to_broadcast([P, 2 * D])).then_inc(a_in, 16)
            with nc.allow_non_contiguous_dma(reason="128 numbers"):
                sp.dma_start(a_c[0:D, :], a_cols).then_inc(a_in, 16)
            sp.dma_start(x_block[:], x_rows[:, 0]).then_inc(x_block_in, 16)
            with sp.Fori(0, NB - 1) as b:
                sp.wait_ge(y_done, b + 1)
                sp.dma_start(out_rows[:, b], y[:]).then_inc(y_out, 16)
                sp.dma_start(x_block[:], x_rows[:, b + 1]).then_inc(x_block_in, 16)
            sp.wait_ge(y_done, NB)
            sp.dma_start(out_rows[:, NB - 1], y[:]).then_inc(y_out, 16)
            sp.wait_ge(y_out, 16 * NB)

        @block.gpsimd
        def _(pool):
            def load(b, it, slot):
                col = it * (BODY * P) + slot * QCOLS
                pool.dma_start(edges[:, slot], adj_rows[:, b, :, bass.ds(col, QCOLS)]).then_inc(slot_in[slot], 16)

            def loads(b, it):
                for slot in range(SLOTS):
                    pool.wait_ge(turn_done, (b * ITERS + it - 1) * SLOTS + slot + 1)
                    load(b, it, slot)

            pool.memset(ident[:], 0.0).then_inc(ident_zero, 1)
            pool.memset(ident_b[:], 0.0).then_inc(ident_zero, 1)
            pool.wait_ge(ident_zero, 2)
            for eye in (ident, ident_b):
                pool.affine_select(out=eye[:], in_=eye[:], compare_op=ALU.not_equal, fill=1.0, base=0,
                                   pattern=[[-1, P]], channel_multiplier=1).then_inc(ident_set, 1)
            for slot in range(SLOTS):
                load(0, 0, slot)
            pool.wait_ge(t_max_ready, 1)
            pool.partition_all_reduce(top[:], t_max[:], P, RMAX).then_inc(top_ready, 1)
            loads(0, 1)
            pool.wait_ge(coef_ready, 4)
            pool.wait_ge(s_ready, 2)
            loads(1, 0)
            combine(pool, 0)
            loads(1, 1)
            attend(pool, 0, first=True)
            with pool.Fori(2, NB) as b:
                loads(b, 0)
                combine(pool, b - 1)
                loads(b, 1)
                attend(pool, b - 1)

        @block.scalar
        def _(act):
            for i in range(2):
                act.wait_ge(centred, i + 1)
                act.activation(prod[:, half[i]], h[:, half[i]], ACT.Square).then_inc(squared, 1)
            act.wait_ge(var_ready, 1)
            act.activation(std[:], var[:], ACT.Sqrt).then_inc(std_ready, 1)
            for g in range(GROUPS):
                act.wait_ge(h_turned, g + 1)
                act.activation(h_t[0:D, g * GCOLS:(g + 1) * GCOLS], halves[g % 2][0:D, :], ACT.Copy,
                               accum_out=hs_part[0:D, g:g + 1]).then_inc(h_t_ready, 1)

            def take_s_row(g):
                act.wait_ge(s_spread, g + 1)
                act.activation(s_row[:, g * GCOLS:(g + 1) * GCOLS], halves[g % 2], ACT.Copy).then_inc(s_row_ready, 1)

            def nearest(i):
                for k, val in ((0, val1), (1, val2)):
                    act.wait_ge(big_ready, 2 * i + k + 1)
                    act.activation(val[:, part[i], 0:W], big[:, k], ACT.Copy, scale=1.0 / LOW).then_inc(near_ready, 1)

            take_s_row(0)
            act.wait_ge(exp_bias, 2)
            act.activation(bexp[:], t[:], ACT.Exp, bias=eb[:, 0:1], scale=1.0).then_inc(exp_ready, 1)
            act.activation(dexp[:], t[:], ACT.Exp, bias=eb[:, 1:2], scale=LEAK).then_inc(exp_ready, 1)
            take_s_row(1)
            nearest(0)
            nearest(1)
            take_s_row(2)
            take_s_row(3)
            act.sem_inc(drained, TILES)
            act.wait_ge(t_big_ready, 1)
            act.wait_ge(s_row_ready, GROUPS)

            def take_block(b, k):
                act.activation(s_block[:, k], s_row[:, bass.ds(b * ROWS, ROWS)], ACT.Copy).then_inc(block_ready, 1)

            def body(b, k, it, first=False, drain_at=None, ahead=True):
                if it == 0:
                    act.wait_ge(block_ready, b + 1)
                for g in range(SLOTS):
                    if it == 1 and g == SLOTS // 2 and ahead:
                        take_block(b + 1, 1 - k)
                    q, r = (b * ITERS + it) * SLOTS + g, g % SIDE_RING
                    if not first or g >= SIDE_RING:
                        act.wait_ge(split_done, q - SIDE_RING + 1)
                    for c in range(QUAD):
                        chunk = it * BODY + g * QUAD + c
                        ins = act.activation(side[:, r, c * ROWS:(c + 1) * ROWS], s_block[:, k],
                                             ACT.Relu, bias=t_big[:, chunk:chunk + 1], scale=BIG)
                    ins.then_inc(side_done, 1)
                    if g == drain_at:
                        drain(b - 1)

            def drain(b):
                for k in range(TILES):
                    if k < TILES - 1:
                        act.wait_ge(tile_done, b * (TILES - 1) + k + 1)
                    else:
                        act.wait_ge(used, (b + 1) * ITERS * SLOTS)
                    act.activation(sums[:, k], acc[:, k, 0:4 * W].rearrange("p (k w) -> p k w", w=W),
                                   ACT.Copy).then_inc(drained, 1)

            take_block(0, 0)
            body(0, 0, 0, first=True)
            nearest(2)
            nearest(3)
            act.wait_ge(row_args, 2)
            act.activation(e1[:], x1[:], ACT.Exp).then_inc(row_exp, 1)
            act.activation(e2[:], x2[:], ACT.Exp).then_inc(row_exp, 1)
            body(0, 0, 1)
            body(1, 1, 0, drain_at=DRAIN_AT)
            body(1, 1, 1)

            def rows(b, k, ahead=True):
                act.wait_ge(att_done, b - 1)
                body(b, k, 0, drain_at=DRAIN_AT)
                body(b, k, 1, ahead=ahead)

            with act.Fori(2, NB - 2, 2) as b:
                rows(b, 0)
                rows(b + 1, 1)
            rows(NB - 2, 0)
            rows(NB - 1, 1, ahead=False)
            act.wait_ge(att_done, NB - 1)
            drain(NB - 1)

        @block.tensor
        def _(pe):
            pe.wait_ge(ident_set, 2)
            for g in range(GROUPS):
                pe.wait_ge(h_ready, g // 2 + 1)
                if g >= 2:
                    pe.wait_ge(h_t_ready, g - 1)
                for c in range(GC):
                    ins = pe.transpose(halves[g % 2][0:D, c * P:(c + 1) * P], h[:, g * GC + c, :], ident[:])
                ins.then_inc(h_turned, 1)
            pe.wait_ge(a_rep_set, 1)
            for g in range(GROUPS):
                pe.wait_ge(h_t_ready, max(g + 1, min(GROUPS, g + 3)))
                if g >= 2:
                    pe.wait_ge(s_row_ready, g - 1)
                for n in range(GCOLS // 512):
                    ins = pe.matmul(halves[g % 2][:, n * 512:(n + 1) * 512], a_rep[0:D, :],
                                    h_t[0:D, g * GCOLS + n * 512:g * GCOLS + (n + 1) * 512], start=True, stop=True)
                ins.then_inc(s_spread, 1)

            def turn(b, it, g):
                pe.wait_ge(slot_in[g], (b * ITERS + it + 1) * 16)
                for c in range(QUAD):
                    for k in range(TILES):
                        o = c * ROWS + k * P
                        ins = pe.transpose(turned[:, g % TURN_RING, o:o + P], edges[:, g, k, c * P:(c + 1) * P],
                                           ident_b[:])
                ins.then_inc(turn_done, 1)

            def add(b, it, g, last_quad):
                pe.wait_ge(split_done, (b * ITERS + it) * SLOTS + g + 1)
                for k in range(TILES):
                    for c in range(QUAD):
                        chunk, o = it * BODY + g * QUAD + c, c * ROWS + k * P
                        for m, val in ((0, val1), (1, val2)):
                            ins = pe.matmul(acc[:, k, m * 2 * W:(m + 1) * 2 * W], split[:, g % SPLIT_RING, m, o:o + P],
                                            val[:, chunk, :], start=False, stop=last_quad and c == QUAD - 1,
                                            skip_group_check=True)
                    if last_quad and k < TILES - 1:
                        ins.then_inc(tile_done, 1)
                ins.then_inc(used, 1)

            def body(b, it, ahead):
                for g in range(SLOTS):
                    n = g + TURN_RING
                    if n < SLOTS or ahead:
                        pe.wait_ge(split_done, (b * ITERS + it) * SLOTS + g + 1)
                        if n < SLOTS:
                            turn(b, it, n)
                        else:
                            turn(*ahead, n - SLOTS)
                    if it == 0 and g == 0:
                        for k in range(TILES):
                            pe.wait_ge(drained, b * TILES + k + 1)
                            pe.matmul(acc[:, k, 0:4 * W], zero_w[:], zero_v[:], start=True, stop=False,
                                      skip_group_check=True)
                    add(b, it, g, it == ITERS - 1 and g == SLOTS - 1)

            pe.wait_ge(s_row_ready, 3)
            for g in range(TURN_RING):
                turn(0, 0, g)
            pe.wait_ge(s_row_ready, 4)
            for c in range(NC):
                pe.matmul(acc[:, 0, c:c + 1], h_t[0:D, c * P:(c + 1) * P], a_c[0:D, 0:1], start=True, stop=True)
            pe.wait_ge(diag_ready, 1)
            pe.matmul(acc[:, 1, 0:D], ones[0:D, :], hs_diag[0:D, :], start=True, stop=True).then_inc(s_cols, 1)
            pe.wait_ge(consts_set, 3)
            pe.wait_ge(s_ready, 2)
            pe.wait_ge(values_ready, 4)
            body(0, 0, (0, 1))
            pe.wait_ge(values_ready, 8)
            body(0, 1, (1, 0))
            with pe.Fori(1, NB - 1) as b:
                body(b, 0, (b, 1))
                body(b, 1, (b + 1, 0))
            body(NB - 1, 0, (NB - 1, 1))
            body(NB - 1, 1, None)

        @block.vector
        def _(v):
            steps = [0]

            def link(ins):
                steps[0] += 1
                ins.then_inc(dve_seq, 1)
                v.wait_ge(dve_seq, steps[0])

            def per_chunk(ap, n):
                return ap.unsqueeze(2).to_broadcast([P, ap.shape[1], n])

            v.memset(zero_w[:], 0.0).then_inc(consts_set, 1)
            v.memset(zero_v[:], 0.0).then_inc(consts_set, 1)
            v.memset(ones[:], 1.0).then_inc(consts_set, 1)
            for i in range(2):
                v.wait_ge(x_in[i], 16)
                link(v.tensor_reduce(mean[:, half[i]], h[:, half[i]], AX.X, ALU.add))
                link(v.tensor_scalar(mean[:, half[i]], mean[:, half[i]], 1.0 / D, None, ALU.mult))
                v.tensor_tensor(h[:, half[i]], h[:, half[i]], per_chunk(mean[:, half[i]], D),
                                ALU.subtract).then_inc(centred, 1)
            for i in range(2):
                v.wait_ge(squared, i + 1)
                link(v.tensor_reduce(var[:, half[i]], prod[:, half[i]], AX.X, ALU.add))
            v.tensor_scalar(var[:], var[:], 1.0 / D, EPS, ALU.mult, ALU.add).then_inc(var_ready, 1)
            v.wait_ge(consts_set, 3)
            v.wait_ge(a_in, 32)
            v.tensor_scalar(a_rep[0:D, :], ones[0:D, :], a_c[0:D, 0:1], None, ALU.mult).then_inc(a_rep_set, 1)
            v.wait_ge(std_ready, 1)
            link(v.reciprocal(quo[:], std[:]))
            link(v.tensor_tensor(quo[:], quo[:], var[:], ALU.mult))
            link(v.tensor_tensor(quo[:], quo[:], std[:], ALU.add))
            link(v.tensor_scalar(quo[:], quo[:], 0.5, None, ALU.mult))
            link(v.reciprocal(rstd[:], quo[:]))
            v.wait_ge(centred, 2)
            for i in range(2):
                v.scalar_tensor_tensor(out=h[:, half[i]], in0=h[:, half[i]], scalar=0.0,
                                       in1=per_chunk(rstd[:, half[i]], D), op0=ALU.max, op1=ALU.mult).then_inc(h_ready, 1)
            v.wait_ge(h_ready, 2)
            link(v.tensor_tensor(prod[:], h[:], a_b[:, D:2 * D].unsqueeze(1).to_broadcast([P, NC, D]), ALU.mult))
            link(v.tensor_reduce(t[:], prod[:], AX.X, ALU.add))
            v.tensor_reduce(t_max[:], t[:], AX.X, ALU.max).then_inc(t_max_ready, 1)
            v.tensor_scalar(t_big[:], t[:], BIG, None, ALU.mult).then_inc(t_big_ready, 1)
            v.wait_ge(h_t_ready, GROUPS)
            link(v.tensor_reduce(hs_col[0:D, :], hs_part[0:D, :], AX.X, ALU.add))
            v.wait_ge(ident_set, 2)
            v.tensor_scalar(hs_diag[0:D, :], ident[0:D, 0:D], hs_col[0:D, 0:1], None, ALU.mult).then_inc(diag_ready, 1)
            v.wait_ge(top_ready, 1)
            v.tensor_scalar(eb[:, 0:1], top[:], -1.0, None, ALU.mult).then_inc(exp_bias, 1)
            v.tensor_scalar(eb[:, 1:2], top[:], -LEAK, None, ALU.mult).then_inc(exp_bias, 1)
            v.wait_ge(exp_ready, 2)
            v.tensor_scalar(bexp[:], bexp[:], SCALE * LOW, None, ALU.mult)
            link(v.tensor_scalar(dexp[:], dexp[:], SCALE * LOW, None, ALU.mult))

            def values(i):
                for k, e in ((0, bexp), (1, dexp)):
                    if i:
                        v.wait_ge(values_ready, 2 * i - 1 + k)
                    v.tensor_copy(big[:, k, :, D], e[:, part[i]])
                    v.tensor_tensor(big[:, k, :, 0:D], h[:, part[i]], per_chunk(e[:, part[i]], D),
                                    ALU.mult).then_inc(big_ready, 1)
                for k, val in ((0, val1), (1, val2)):
                    v.wait_ge(near_ready, 2 * i + k + 1)
                    v.scalar_tensor_tensor(out=val[:, part[i], W:2 * W], in0=val[:, part[i], 0:W], scalar=-LOW,
                                           in1=big[:, k], op0=ALU.mult, op1=ALU.add).then_inc(values_ready, 1)

            values(0)
            values(1)

            def body(b, it, first=False, invert_at=None, finish_at=None, early=False):
                for g in range(SLOTS):
                    q, r = (b * ITERS + it) * SLOTS + g, g % SPLIT_RING
                    edge = turned[:, g % TURN_RING].bitcast(F16)
                    v.wait_ge(turn_done, q + 1)
                    v.wait_ge(side_done, q + 1)
                    if not first or g >= SPLIT_RING:
                        v.wait_ge(used, q - SPLIT_RING + 1)
                    v.tensor_tensor(split[:, r, 1], edge, side[:, g % SIDE_RING], ALU.is_gt).then_inc(neg_done, 1)
                    v.wait_ge(neg_done, q + 1)
                    v.tensor_tensor(split[:, r, 0], edge, split[:, r, 1].bitcast(I16), ALU.is_gt).then_inc(split_done, 1)
                    if g == invert_at:
                        invert(b - 1)
                    if g == finish_at:
                        if not early:
                            v.wait_ge(y_out, 16 * (b - 1))
                        finish(b - 1)

            def invert(b):
                v.wait_ge(combined, b + 1)
                v.tensor_scalar(lone[:], total[:, :, D], 0.0, None, ALU.is_equal).then_inc(inv_done, 1)
                v.wait_ge(inv_done, 3 * b + 1)
                v.scalar_tensor_tensor(out=den[:], in0=lone[:], scalar=float(N), in1=total[:, :, D], op0=ALU.mult,
                                       op1=ALU.add).then_inc(inv_done, 1)
                v.wait_ge(inv_done, 3 * b + 2)
                v.reciprocal(inv[:], den[:]).then_inc(inv_done, 1)

            def finish(b):
                v.wait_ge(att_done, b + 1)
                v.wait_ge(x_block_in, 16 * (b + 1))
                v.scalar_tensor_tensor(out=y[:], in0=att[:], scalar=0.0, in1=x_block[:],
                                       op0=ALU.max, op1=ALU.add).then_inc(y_done, 1)

            v.wait_ge(s_cols, 1)
            v.tensor_copy(s[:], acc[:, 0, 0:NC]).then_inc(s_ready, 1)
            v.tensor_copy(h_sum[:], acc[:, 1, 0:D]).then_inc(s_ready, 1)
            body(0, 0, first=True)
            values(2)
            values(3)
            v.wait_ge(s_ready, 2)
            link(v.tensor_scalar(xs[:], s[:], top[:, 0:1], None, ALU.add))
            link(v.scalar_tensor_tensor(out=xm[:], in0=xs[:], scalar=LEAK, in1=xs[:], op0=ALU.mult, op1=ALU.max))
            v.tensor_tensor(x1[:], xs[:], xm[:], ALU.subtract).then_inc(row_args, 1)
            v.scalar_tensor_tensor(out=x2[:], in0=xs[:], scalar=LEAK, in1=xm[:], op0=ALU.mult,
                                   op1=ALU.subtract).then_inc(row_args, 1)
            v.wait_ge(row_exp, 2)
            for k, e in ((0, e1), (2, e2)):
                v.tensor_copy(coef[:, :, k], e[:]).then_inc(coef_ready, 1)
                v.tensor_scalar(coef[:, :, k + 1], e[:], 1.0 / LOW, None, ALU.mult).then_inc(coef_ready, 1)
            body(0, 1)
            body(1, 0)
            body(1, 1, invert_at=1, finish_at=3, early=True)
            with v.Fori(2, NB) as b:
                body(b, 0)
                body(b, 1, invert_at=1, finish_at=3)
            combine(v, NB - 1)
            invert(NB - 1)
            attend(v, NB - 1)
            v.wait_ge(y_out, 16 * (NB - 1))
            finish(NB - 1)
    return nc


DRAIN_AT = 1


def kernel(**inputs):
    import numpy as _np
    import concourse.bacc as _bacc
    from concourse import mybir as _mybir
    from concourse.bass_utils import run_bass_kernel_spmd as _run

    nc = _bacc.Bacc("TRN2", target_bir_lowering=False, num_devices=1)
    arrays, args = {}, []
    for name in ("x", "adj", "L0_gnn_a"):
        v = _np.ascontiguousarray(inputs[name])
        arrays[f"in_{name}"] = v
        args.append(nc.dram_tensor(f"in_{name}", v.shape, _mybir.dt.from_np(v.dtype), kind="ExternalInput").ap())
    out = nc.dram_tensor("out", inputs["x"].shape, _mybir.dt.float32, kind="ExternalOutput").ap()
    gat_layer(nc, *args, out)
    r = _run(nc, [arrays], core_ids=[0])
    return r.results[0]["out"]
```

```python
from contextlib import ExitStack

import concourse.bass as bass
from concourse import mybir

ALU = mybir.AluOpType
ACT = mybir.ActivationFunctionType
AX = mybir.AxisListType
F32 = mybir.dt.float32
BF16 = mybir.dt.bfloat16
F16 = mybir.dt.float16
I16 = mybir.dt.int16
I32 = mybir.dt.int32
RMAX = bass.bass_isa.ReduceOp.max


P = 128
LEAK = 0.2
EPS = 1e-5
BIG = 2.0 ** 64
LOW = 2.0 ** 11
SCALE = 2.0 ** 12

TILES = 4
ROWS = TILES * P
QUAD = 4
QCOLS = QUAD * P
SPAN = 10.0
SLOTS = 8
DRAIN_AT = 2
TURN_RING = 2
SIDE_RING = 4
SPLIT_RING = 4
GROUPS = 8
PART = 16
CONSTS = 4
ROW_TAKERS = ["act", "act", "act", "act", "act", "dve", "dve", "dve"]


def gat_layer(nc, x, adj, a, out):
    N, D = x.shape
    NC = N // P
    NB = N // ROWS
    W = D + 1
    BODY = SLOTS * QUAD
    ITERS = NC // BODY
    GC = NC // GROUPS
    GCOLS = GC * P
    H_STEPS = NC.bit_length() - 1
    assert ITERS * BODY == NC and GCOLS == 1024 and ITERS == 2 and TILES == QUAD

    x_cols = x.rearrange("(q p c) d -> p q c d", p=P, c=QUAD)
    out_rows = out.rearrange("(b p t) d -> p b t d", p=P, t=TILES)
    x_rows = x.rearrange("(b p t) d -> p b t d", p=P, t=TILES)
    adj_rows = adj.rearrange("(b p t) j -> p b t j", p=P, t=TILES)
    a_row = a.rearrange("k o -> o k")

    with ExitStack() as ctx:
        def sb(name, shape, dt=F32):
            return ctx.enter_context(nc.sbuf_tensor(name, [P] + shape, dt))

        def sem(name):
            return ctx.enter_context(nc.semaphore(name))

        turned = ctx.enter_context(nc.psum_tensor("turned", [P, TURN_RING, QUAD * ROWS], BF16))
        acc = ctx.enter_context(nc.psum_tensor("acc", [P, TILES, 512], F32))
        h_psum = acc[:, TILES - 1, 4 * W:4 * W + D]
        s_psum = acc[:, TILES - 1, 0:P].bitcast(BF16)
        row_psum = acc[:].rearrange("p t n -> p (t n)")

        h = sb("h", [NC, D])
        x_block = sb("x_block", [TILES, D])
        ident = sb("ident", [P])
        ident_b = sb("ident_b", [P], BF16)
        s_row = sb("s_row", [N])
        s_block = sb("s_block", [2, ROWS])
        t = sb("t", [NC])
        t_big = sb("t_big", [NC])
        val1 = sb("val1", [NC, 2 * W], F16)
        val2 = sb("val2", [NC, 2 * W], F16)
        coef = sb("coef", [NC, 4])
        h_sum = sb("h_sum", [D])
        zero_w = sb("zero_w", [P], BF16)
        zero_v = sb("zero_v", [W], BF16)
        edges = sb("edges", [SLOTS, TILES, QCOLS], BF16)
        side = sb("side", [SIDE_RING, QUAD * ROWS], BF16)
        split = sb("split", [SPLIT_RING, 2, QUAD * ROWS], BF16)
        sums = sb("sums", [TILES, 4, W])
        comb = sb("comb", [TILES, 2, W])
        total = sb("total", [TILES, W])
        lone = sb("lone", [TILES])
        fill = sb("fill", [TILES, D])
        filled = sb("filled", [TILES, D])
        den = sb("den", [TILES])
        inv = sb("inv", [TILES])
        att = sb("att", [TILES, D])
        y = sb("y", [TILES, D])
        big = sb("big", [2, 2, PART, W])
        prod = side[:].rearrange("p r n -> p (r n)").bitcast(F32).rearrange("p (c d) -> p c d", d=D)
        prod_t = split[:].rearrange("p r k n -> p (r k n)").bitcast(F32)[:, 0:NC * D].rearrange("p (c d) -> p c d", d=D)
        h_halved = split[:].rearrange("p r k n -> p (r k n)").bitcast(F32)[:, NC * D:NC * D * 3 // 2].rearrange(
            "p (c d) -> p c d", d=D)
        a_b = sb("a_b", [2 * D])
        s_parts = sb("s_parts", [3, NC], BF16)
        s_left = sb("s_left", [NC])
        s_t = sb("s_t", [2, P], BF16)
        pick = sb("pick", [NC], BF16)
        low = sb("low", [1])
        ones = sb("ones", [P])
        mean = sb("mean", [NC])
        var = sb("var", [NC])
        std = sb("std", [NC])
        quo = sb("quo", [NC])
        rstd = sb("rstd", [NC])
        s = sb("s", [NC])
        h_part = sb("h_part", [D])
        s_raw = sb("s_raw", [NC])
        t_raw = sb("t_raw", [NC])
        ext = sb("ext", [2])
        top = sb("top", [2])
        wide = sb("wide", [1])
        wide_i = sb("wide_i", [1], I32)
        neg_t = sb("neg_t", [NC])
        eb = sb("eb", [2])
        bexp = sb("bexp", [NC])
        dexp = sb("dexp", [NC])
        bexp_2 = sb("bexp_2", [NC])
        dexp_2 = sb("dexp_2", [NC])
        xs, xm, x1, x2 = mean, var, std, quo
        e1 = sb("e1", [NC])
        e2 = sb("e2", [NC])

        x_in = [sem(f"x_in{i}") for i in range(3)]
        a_in = sem("a_in")
        ident_zero = sem("ident_zero")
        ident_set = sem("ident_set")
        consts_set = sem("consts_set")
        centred = sem("centred")
        kept = sem("kept")
        squared = sem("squared")
        var_ready = sem("var_ready")
        std_ready = sem("std_ready")
        table_in = sem("table_in")
        prod_ready = sem("prod_ready")
        rstd_ready = sem("rstd_ready")
        h_ready = sem("h_ready")
        prod_t_ready = sem("prod_t_ready")
        h_parts = sem("h_parts")
        h_added = sem("h_added")
        h_sum_ready = sem("h_sum_ready")
        parts_ready = sem("parts_ready")
        pick_ready = sem("pick_ready")
        s_turned = sem("s_turned")
        s_t_ready = sem("s_t_ready")
        s_spread = sem("s_spread")
        s_row_ready = {e: sem(f"s_row_ready_{e}") for e in ("act", "dve")}
        t_big_ready = sem("t_big_ready")
        ext_ready = sem("ext_ready")
        top_ready = sem("top_ready")
        wide_ready = sem("wide_ready")
        exp_bias = sem("exp_bias")
        exp_ready = sem("exp_ready")
        exp_scaled = sem("exp_scaled")
        big_ready = [sem(f"big_ready{i}") for i in range(NC // PART)]
        near_ready = [sem(f"near_ready{i}") for i in range(NC // PART)]
        values_ready = sem("values_ready")
        rest_seq = sem("rest_seq")
        rests_ready = sem("rests_ready")
        row_args = sem("row_args")
        row_exp = sem("row_exp")
        coef_ready = sem("coef_ready")
        dve_seq = sem("dve_seq")

        slot_in = [sem(f"slot_in{i}") for i in range(SLOTS)]
        block_ready = sem("block_ready")
        turn_done = sem("turn_done")
        side_done = sem("side_done")
        neg_done = sem("neg_done")
        split_done = sem("split_done")
        used = sem("used")
        tile_done = sem("tile_done")
        drained = sem("drained")
        comb_seq = sem("comb_seq")
        combined = sem("combined")
        inv_done = sem("inv_done")
        x_block_in = sem("x_block_in")
        att_done = sem("att_done")
        y_done = sem("y_done")
        y_out = sem("y_out")

        half = [slice(0, NC // 2), slice(NC // 2, NC)]
        pieces = [slice(0, NC // 4), slice(NC // 4, NC // 2), slice(NC // 2, NC)]
        part = [slice(i, i + PART) for i in range(0, NC, PART)]

        def s_row_group(g):
            return s_row[:, g * GCOLS:(g + 1) * GCOLS], row_psum[:, g % 2 * GCOLS:(g % 2 + 1) * GCOLS]

        def wait_s_row(eng, upto):
            for e, sem_e in s_row_ready.items():
                n = sum(taker == e for taker in ROW_TAKERS[:upto])
                if n:
                    eng.wait_ge(sem_e, n)

        def make_big(eng, i):
            for k, e in ((0, bexp), (1, dexp)) if i < 2 else ((0, bexp_2), (1, dexp_2)):
                if i >= 2:
                    eng.wait_ge(values_ready, 2 * (i - 2) + k + 1)
                eng.tensor_copy(big[:, i % 2, k, :, D], e[:, part[i]])
                eng.tensor_tensor(big[:, i % 2, k, :, 0:D], h[:, part[i]],
                                  e[:, part[i]].unsqueeze(2).to_broadcast([P, PART, D]),
                                  ALU.mult).then_inc(big_ready[i], 1)

        def flat(ap):
            return ap.rearrange("p a b c -> p (a b c)").bitcast(F32)

        room = flat(split[:])
        run, marked, m_row, score = (room[:, i * ROWS:(i + 1) * ROWS] for i in range(4))
        weight, prob, diag, leaky = (room[:, i * ROWS:(i + 1) * ROWS] for i in range(4, 8))
        small = room[:, 8 * ROWS:8 * ROWS + 512]
        lift_t, up, down, peak = small[:, 0:NC], small[:, NC:NC + 1], small[:, NC + 1:NC + 2], small[:, 80:80 + TILES]
        row_m = small[:, 96:96 + TILES]
        g_edges = edges[:, SLOTS - 1]
        g_turned = turned[:, 0, 0:ROWS]
        QUADS = NC // QUAD

        g_in = sem("g_in")
        g_turn = sem("g_turn")
        g_read = sem("g_read")
        g_prep = sem("g_prep")
        g_clear = sem("g_clear")
        g_max = sem("g_max")
        g_run = sem("g_run")
        g_mid = sem("g_mid")
        g_spread = sem("g_spread")
        g_score = sem("g_score")
        g_exp = sem("g_exp")
        g_used = sem("g_used")
        g_end = sem("g_end")
        g_x = sem("g_x")
        g_out = sem("g_out")
        g_y_free = sem("g_y_free")

        def general_sp(sp):
            sp.sem_inc(g_y_free, 1)
            with sp.Fori(0, NB) as b:
                sp.wait_ge(g_y_free, b + 1)
                sp.dma_start(x_block[:], x_rows[:, b]).then_inc(g_x, 16)
                sp.wait_ge(g_end, 8 * (b + 1))
                sp.dma_start(out_rows[:, b], y[:]).then_inc(g_out, 16)
                sp.wait_ge(g_out, 16 * (b + 1))
                sp.sem_inc(g_y_free, 1)

        def general_pool(pool):
            pool.wait_ge(slot_in[SLOTS - 1], 16)
            with pool.Fori(0, NB) as b:
                for half_pass in range(2):
                    with pool.Fori(0, QUADS) as u:
                        pool.wait_ge(g_turn, ((b * 2 + half_pass) * QUADS + u + 1) * QUAD)
                        pool.dma_start(g_edges, adj_rows[:, b, :, bass.ds(u * QCOLS, QCOLS)]).then_inc(g_in, 16)

        def general_act(act):
            with act.Fori(0, NB * NC) as n:
                act.wait_ge(g_score, 4 * n + 4)
                act.activation(weight, score, ACT.Exp).then_inc(g_exp, 1)

        def general_pe(pe):
            pe.sem_inc(g_turn, QUAD)
            pe.sem_inc(g_used, 1)

            def turn_chunk(b, half_pass, u, c):
                pe.wait_ge(g_read, ((b * 2 + half_pass) * QUADS + u) * QUAD + c + 1)
                for k in range(TILES):
                    ins = pe.transpose(g_turned[:, k * P:(k + 1) * P], g_edges[:, k, c::QUAD], ident_b[:])
                ins.then_inc(g_turn, 1)

            with pe.Fori(0, NB) as b:
                with pe.Fori(0, QUADS) as u:
                    pe.wait_ge(g_in, (b * 2 * QUADS + u + 1) * 16)
                    for c in range(QUAD):
                        turn_chunk(b, 0, u, c)
                pe.wait_ge(g_max, (b + 1) * NC + 1)
                for k in range(TILES):
                    ins = pe.transpose(acc[:, k, 0:P], run[:, k * P:(k + 1) * P], ident[:])
                ins.then_inc(g_run, 1)
                pe.wait_ge(g_mid, 8 * b + 7)
                for k in range(TILES):
                    ins = pe.matmul(acc[:, k, P:2 * P], ones[:], diag[:, k * P:(k + 1) * P], start=True, stop=True)
                ins.then_inc(g_spread, 1)
                pe.wait_ge(g_mid, 8 * b + 8)
                for k in range(TILES):
                    pe.matmul(acc[:, k, 0:W], zero_w[:], zero_v[:], start=True, stop=False, skip_group_check=True)
                with pe.Fori(0, QUADS) as u:
                    pe.wait_ge(g_in, ((b * 2 + 1) * QUADS + u + 1) * 16)
                    for c in range(QUAD):
                        turn_chunk(b, 1, u, c)
                        pe.wait_ge(g_read, ((b * 2 + 1) * QUADS + u) * QUAD + c + 2)
                        for k in range(TILES):
                            lhs = prob[:, k * P:(k + 1) * P]
                            pe.matmul(acc[:, k, 0:D], lhs, h[:, bass.ds(u * QUAD + c, 1), :].squeeze(1), start=False,
                                      stop=False, skip_group_check=True)
                            ins = pe.matmul(acc[:, k, D:W], lhs, ones[:, 0:1], start=False, stop=False,
                                            skip_group_check=True)
                        ins.then_inc(g_used, 1)

        def general_v(v):
            v.wait_ge(h_sum_ready, 1)
            v.sem_inc(g_read, 1)
            v.sem_inc(g_max, 1)
            v.tensor_scalar(up, top[:, 1:2], 1.0, None, ALU.add).then_inc(g_prep, 1)
            v.wait_ge(g_prep, 1)
            v.tensor_scalar(down, up, -1.0, None, ALU.mult).then_inc(g_prep, 1)
            v.tensor_scalar(lift_t, t[:], up, None, ALU.add).then_inc(g_prep, 1)
            v.wait_ge(g_prep, 3)
            with v.Fori(0, NB) as b:
                v.memset(run, 0.0).then_inc(g_clear, 1)
                with v.Fori(0, QUADS) as u:
                    v.wait_ge(g_clear, b + 1)
                    for c in range(QUAD):
                        n, chunk = (b * 2 * QUADS + u) * QUAD + c, b * NC + u * QUAD + c
                        v.wait_ge(g_turn, n + 1 + QUAD)
                        v.wait_ge(g_max, chunk + 1)
                        v.tensor_scalar(marked, g_turned, 0.0, lift_t[:, bass.ds(u * QUAD + c, 1)], ALU.is_gt,
                                        ALU.mult).then_inc(g_read, 1)
                        v.wait_ge(g_read, n + 2)
                        v.tensor_tensor(run, run, marked, ALU.max).then_inc(g_max, 1)
                v.wait_ge(g_run, b + 1)
                v.tensor_reduce(peak, acc[:, :, 0:P], AX.X, ALU.max).then_inc(g_mid, 1)
                v.wait_ge(g_mid, 8 * b + 1)
                v.scalar_tensor_tensor(out=row_m, in0=peak, scalar=down, in1=s[:, bass.ds(b * TILES, TILES)],
                                       op0=ALU.add, op1=ALU.add).then_inc(g_mid, 1)
                v.wait_ge(g_mid, 8 * b + 2)
                v.scalar_tensor_tensor(out=peak, in0=row_m, scalar=LEAK, in1=row_m, op0=ALU.mult,
                                       op1=ALU.max).then_inc(g_mid, 1)
                v.wait_ge(g_mid, 8 * b + 3)
                for k in range(TILES):
                    v.tensor_scalar(diag[:, k * P:(k + 1) * P], ident[:], peak[:, k:k + 1], None,
                                    ALU.mult).then_inc(g_mid, 1)
                v.wait_ge(g_spread, b + 1)
                v.tensor_copy(m_row.rearrange("p (k n) -> p k n", k=TILES), acc[:, :, P:2 * P]).then_inc(g_mid, 1)
                with v.Fori(0, QUADS) as u:
                    v.wait_ge(g_mid, 8 * b + 8)
                    for c in range(QUAD):
                        n, chunk = ((b * 2 + 1) * QUADS + u) * QUAD + c, b * NC + u * QUAD + c
                        step = 4 * chunk
                        v.wait_ge(g_read, n + 1)
                        v.tensor_scalar(leaky, s_row[:, bass.ds(b * ROWS, ROWS)], t[:, bass.ds(u * QUAD + c, 1)], None,
                                        ALU.add).then_inc(g_score, 1)
                        v.wait_ge(g_score, step + 1)
                        v.scalar_tensor_tensor(out=score, in0=leaky, scalar=LEAK, in1=leaky, op0=ALU.mult,
                                               op1=ALU.max).then_inc(g_score, 1)
                        v.wait_ge(g_score, step + 2)
                        v.tensor_tensor(leaky, score, m_row, ALU.subtract).then_inc(g_score, 1)
                        v.wait_ge(g_score, step + 3)
                        v.tensor_scalar(score, leaky, 1.0, None, ALU.min).then_inc(g_score, 1)
                        v.wait_ge(g_exp, chunk + 1)
                        v.wait_ge(g_turn, n + 1 + QUAD)
                        v.wait_ge(g_used, chunk + 1)
                        v.scalar_tensor_tensor(out=prob, in0=g_turned, scalar=0.0, in1=weight, op0=ALU.is_gt,
                                               op1=ALU.mult).then_inc(g_read, 1)
                v.wait_ge(g_used, (b + 1) * NC + 1)
                v.tensor_copy(total[:], acc[:, :, 0:W]).then_inc(g_end, 1)
                v.wait_ge(g_end, 8 * b + 1)
                v.tensor_scalar(lone[:], total[:, :, D], 0.0, None, ALU.is_equal).then_inc(g_end, 1)
                v.wait_ge(g_end, 8 * b + 2)
                v.scalar_tensor_tensor(out=den[:], in0=lone[:], scalar=float(N), in1=total[:, :, D], op0=ALU.mult,
                                       op1=ALU.add).then_inc(g_end, 1)
                v.tensor_tensor(fill[:], h_sum[:].unsqueeze(1).to_broadcast([P, TILES, D]),
                                lone[:].unsqueeze(2).to_broadcast([P, TILES, D]), ALU.mult).then_inc(g_end, 1)
                v.wait_ge(g_end, 8 * b + 4)
                v.reciprocal(inv[:], den[:]).then_inc(g_end, 1)
                v.tensor_tensor(filled[:], total[:, :, 0:D], fill[:], ALU.add).then_inc(g_end, 1)
                v.wait_ge(g_end, 8 * b + 6)
                v.tensor_tensor(att[:], filled[:], inv[:].unsqueeze(2).to_broadcast([P, TILES, D]),
                                ALU.mult).then_inc(g_end, 1)
                v.wait_ge(g_end, 8 * b + 7)
                v.wait_ge(g_x, 16 * (b + 1))
                v.wait_ge(g_y_free, b + 1)
                v.scalar_tensor_tensor(out=y[:], in0=att[:], scalar=0.0, in1=x_block[:], op0=ALU.max,
                                       op1=ALU.add).then_inc(g_end, 1)

        block = ctx.enter_context(nc.Block())

        @block.sync
        def _(sp):
            for i, piece in enumerate(pieces):
                sp.dma_start(h[:, piece].rearrange("p (q c) d -> p q c d", c=QUAD),
                             x_cols[:, piece.start // QUAD:piece.stop // QUAD]).then_inc(x_in[i], 16)
            sp.dma_start(a_b[:], a_row.to_broadcast([P, 2 * D])).then_inc(a_in, 16)
            sp.wait_ge(wide_ready, 1)
            with sp.If(sp.value_load(wide_i[0:1, 0:1], min_val=0, max_val=1) == 0):
                sp.dma_start(x_block[:], x_rows[:, 0]).then_inc(x_block_in, 16)
                with sp.Fori(0, NB - 1) as b:
                    sp.wait_ge(y_done, b + 1)
                    sp.dma_start(out_rows[:, b], y[:]).then_inc(y_out, 16)
                    sp.dma_start(x_block[:], x_rows[:, b + 1]).then_inc(x_block_in, 16)
                sp.wait_ge(y_done, NB)
                sp.dma_start(out_rows[:, NB - 1], y[:]).then_inc(y_out, 16)
                sp.wait_ge(y_out, 16 * NB)
            with sp.Else():
                general_sp(sp)

        @block.gpsimd
        def _(pool):
            def load(b, it, slot):
                col = it * (BODY * P) + slot * QCOLS
                pool.dma_start(edges[:, slot], adj_rows[:, b, :, bass.ds(col, QCOLS)]).then_inc(slot_in[slot], 16)

            def loads(b, it, slots=range(SLOTS)):
                for slot in slots:
                    pool.wait_ge(turn_done, (b * ITERS + it - 1) * SLOTS + slot + 1)
                    load(b, it, slot)

            def combine(b):
                seq = b * 4
                cf = coef[:, bass.ds(b * TILES, TILES), :].unsqueeze(3).to_broadcast([P, TILES, 4, W])
                pool.wait_ge(drained, (b + 2) * TILES)
                pool.tensor_tensor(sums[:], sums[:], cf, ALU.mult).then_inc(comb_seq, 1)
                pool.wait_ge(comb_seq, seq + 1)
                pool.tensor_tensor(comb[:], sums[:, :, 0:2], sums[:, :, 2:4], ALU.add).then_inc(comb_seq, 1)
                pool.wait_ge(comb_seq, seq + 2)
                pool.tensor_tensor(total[:], comb[:, :, 0], comb[:, :, 1], ALU.add).then_inc(combined, 1)

            def attend(b, first=False):
                seq = b * 4
                pool.wait_ge(inv_done, (b + 1) * 3)
                pool.tensor_tensor(fill[:], h_sum[:].unsqueeze(1).to_broadcast([P, TILES, D]),
                                  lone[:].unsqueeze(2).to_broadcast([P, TILES, D]), ALU.mult).then_inc(comb_seq, 1)
                pool.wait_ge(comb_seq, seq + 3)
                pool.tensor_tensor(filled[:], total[:, :, 0:D], fill[:], ALU.add).then_inc(comb_seq, 1)
                pool.wait_ge(comb_seq, seq + 4)
                if not first:
                    pool.wait_ge(y_done, b)
                pool.tensor_tensor(att[:], filled[:], inv[:].unsqueeze(2).to_broadcast([P, TILES, D]),
                                  ALU.mult).then_inc(att_done, 1)

            def add_half(i):
                n = NC // 4
                pool.tensor_tensor(h_halved[:, i * n:(i + 1) * n], h[:, i * n:(i + 1) * n],
                                   h[:, (i + 2) * n:(i + 3) * n], ALU.add).then_inc(h_parts, 1)

            def add_chunks():
                n = NC // 2
                for i in range(1, H_STEPS):
                    n //= 2
                    pool.wait_ge(h_parts, i + 1)
                    dst = h_part[:].unsqueeze(1) if n == 1 else h_halved[:, 0:n]
                    pool.tensor_tensor(dst, h_halved[:, 0:n], h_halved[:, n:2 * n], ALU.add).then_inc(h_parts, 1)

            pool.memset(ident[:], 0.0).then_inc(ident_zero, 1)
            pool.memset(ident_b[:], 0.0).then_inc(ident_zero, 1)
            pool.wait_ge(ident_zero, 2)
            for eye in (ident, ident_b):
                pool.affine_select(out=eye[:], in_=eye[:], compare_op=ALU.not_equal, fill=1.0, base=0,
                                   pattern=[[-1, P]], channel_multiplier=1).then_inc(ident_set, 1)
            for slot in range(SLOTS):
                load(0, 0, slot)
            loads(0, 1, range(TURN_RING))
            pool.wait_ge(a_in, 16)
            for i in range(2):
                pool.wait_ge(kept, i + 1)
                pool.tensor_tensor(prod_t[:, half[i]], h[:, half[i]],
                                   a_b[:, D:2 * D].unsqueeze(1).to_broadcast([P, NC // 2, D]),
                                   ALU.mult).then_inc(prod_t_ready, 1)
            pool.wait_ge(rstd_ready, 1)
            pool.wait_ge(prod_ready, 1)
            pool.wait_ge(prod_t_ready, 2)
            for i in range(2):
                pool.tensor_tensor(h[:, half[i]], h[:, half[i]],
                                   rstd[:, half[i]].unsqueeze(2).to_broadcast([P, NC // 2, D]),
                                   ALU.mult).then_inc(h_ready, 1)
            pool.wait_ge(h_ready, 2)
            add_half(0)
            pool.wait_ge(ext_ready, 2)
            pool.partition_all_reduce(top[:], ext[:], P, RMAX).then_inc(top_ready, 1)
            add_half(1)

            pool.wait_ge(exp_scaled, 4)
            make_big(pool, 1)
            add_chunks()
            pool.wait_ge(wide_ready, 1)
            with pool.If(pool.value_load(wide_i[0:1, 0:1], min_val=0, max_val=1) == 0):
                def pool_rest(i):
                    for k, val in ((0, val1), (1, val2)):
                        kind = big[:, i % 2, k]
                        pool.wait_ge(near_ready[i], k + 1)
                        pool.tensor_tensor(kind, kind, val[:, part[i], 0:W], ALU.subtract).then_inc(rest_seq, 1)
                        pool.wait_ge(rest_seq, 2 * (i - 2) + k + 1)
                        pool.tensor_tensor(val[:, part[i], W:2 * W], kind,
                                           low[:].unsqueeze(2).to_broadcast([P, PART, W]),
                                           ALU.mult).then_inc(rests_ready, 1)

                make_big(pool, 2)
                loads(0, 1, (2,))
                make_big(pool, 3)
                loads(0, 1, (3, 4, 5))
                pool_rest(2)
                loads(0, 1, (6, 7))
                pool_rest(3)
                loads(1, 0)
                pool.wait_ge(coef_ready, 4)
                combine(0)
                loads(1, 1)
                pool.wait_ge(h_sum_ready, 1)
                attend(0, first=True)
                with pool.Fori(2, NB) as b:
                    loads(b, 0)
                    combine(b - 1)
                    loads(b, 1)
                    attend(b - 1)
            with pool.Else():
                general_pool(pool)

        @block.scalar
        def _(act):
            for i in range(2):
                act.wait_ge(centred, i + 1)
                act.activation(prod[:, half[i]], h[:, half[i]], ACT.Square).then_inc(squared, 1)
                act.wait_ge(squared, i + 1)
                act.activation(h[:, half[i]], h[:, half[i]], ACT.Relu).then_inc(kept, 1)
            act.wait_ge(var_ready, 1)
            act.activation(std[:], var[:], ACT.Sqrt).then_inc(std_ready, 1)
            act.wait_ge(consts_set, CONSTS)
            act.activation(wide[:], ones[:, 0:1], ACT.Exp).then_inc(table_in, 1)

            def take_s_row(g):
                dst, src = s_row_group(g)
                act.wait_ge(s_spread, g + 1)
                act.activation(dst, src, ACT.Copy).then_inc(s_row_ready["act"], 1)

            def take_h_sum():
                act.wait_ge(h_added, 1)
                act.activation(h_sum[:], h_psum, ACT.Copy).then_inc(h_sum_ready, 1)

            def take_block(b, k):
                act.activation(s_block[:, k], s_row[:, bass.ds(b * ROWS, ROWS)], ACT.Copy).then_inc(block_ready, 1)

            def nearest(i):
                for k, val in ((0, val1), (1, val2)):
                    act.wait_ge(big_ready[i], k + 1)
                    act.activation(val[:, part[i], 0:W], big[:, i % 2, k], ACT.Copy,
                                   scale=1.0 / LOW if i < 2 else 1.0).then_inc(near_ready[i], 1)

            act.wait_ge(s_turned, 1)
            act.activation(s_t[:, 0, :], s_psum[:, 0:P], ACT.Copy).then_inc(s_t_ready, 1)
            act.activation(s_t[0:NC, 1, :], s_psum[0:NC, P:2 * P], ACT.Copy).then_inc(s_t_ready, 1)
            take_s_row(0)
            act.wait_ge(s_row_ready["act"], 1)
            take_block(0, 0)
            take_s_row(1)
            act.wait_ge(exp_bias, 2)
            act.activation(bexp[:], t[:], ACT.Exp, bias=eb[:, 0:1], scale=1.0).then_inc(exp_ready, 1)
            act.activation(dexp[:], t[:], ACT.Exp, bias=eb[:, 1:2], scale=LEAK).then_inc(exp_ready, 1)
            take_s_row(2)
            take_s_row(3)
            nearest(0)
            take_s_row(4)
            act.wait_ge(wide_ready, 1)
            with act.If(act.value_load(wide_i[0:1, 0:1], min_val=0, max_val=1) == 0):
                act.sem_inc(drained, TILES)
                act.wait_ge(t_big_ready, 1)

                def body(b, k, it, first=False, drain_at=None, ahead=True, between=None):
                    if it == 0:
                        act.wait_ge(block_ready, b + 1)
                    for g in range(SLOTS):
                        if it == 1 and g == SLOTS // 2 and ahead:
                            take_block(b + 1, 1 - k)
                        q, r = (b * ITERS + it) * SLOTS + g, g % SIDE_RING
                        if not first or g >= SIDE_RING:
                            act.wait_ge(split_done, q - SIDE_RING + 1)
                        for c in range(QUAD):
                            chunk = it * BODY + g * QUAD + c
                            ins = act.activation(side[:, r, c * ROWS:(c + 1) * ROWS], s_block[:, k],
                                                 ACT.Relu, bias=t_big[:, chunk:chunk + 1], scale=BIG)
                        ins.then_inc(side_done, 1)
                        if g == drain_at:
                            drain(b - 1)
                        if between and g in between:
                            between[g]()

                def drain(b, first=False):
                    for k in range(TILES):
                        if first and k == TILES - 1:
                            take_h_sum()
                        if k < TILES - 1:
                            act.wait_ge(tile_done, b * (TILES - 1) + k + 1)
                        else:
                            act.wait_ge(used, (b + 1) * ITERS * SLOTS)
                        act.activation(sums[:, k], acc[:, k, 0:4 * W].rearrange("p (k w) -> p k w", w=W),
                                       ACT.Copy).then_inc(drained, 1)

                def row_exps():
                    act.wait_ge(row_args, 2)
                    act.activation(e1[:], x1[:], ACT.Exp).then_inc(row_exp, 1)
                    act.activation(e2[:], x2[:], ACT.Exp).then_inc(row_exp, 1)

                body(0, 0, 0, first=True, between={1: lambda: nearest(1), 3: lambda: nearest(2), 6: lambda: nearest(3)})
                wait_s_row(act, GROUPS)
                body(0, 0, 1, between={3: row_exps})
                body(1, 1, 0, between={DRAIN_AT: lambda: drain(0, first=True)})
                body(1, 1, 1)

                def rows(b, k, ahead=True):
                    act.wait_ge(att_done, b - 1)
                    body(b, k, 0, drain_at=DRAIN_AT)
                    body(b, k, 1, ahead=ahead)

                with act.Fori(2, NB - 2, 2) as b:
                    rows(b, 0)
                    rows(b + 1, 1)
                rows(NB - 2, 0)
                rows(NB - 1, 1, ahead=False)
            with act.Else():
                nearest(1)
                take_h_sum()
                general_act(act)

        @block.tensor
        def _(pe):
            pe.wait_ge(ident_set, 2)

            def turn(b, it, g):
                pe.wait_ge(slot_in[g], (b * ITERS + it + 1) * 16)
                for c in range(QUAD):
                    for k in range(TILES):
                        o = c * ROWS + k * P
                        ins = pe.transpose(turned[:, g % TURN_RING, o:o + P], edges[:, g, k, c::QUAD], ident_b[:])
                ins.then_inc(turn_done, 1)

            def add(b, it, g, last_quad):
                pe.wait_ge(split_done, (b * ITERS + it) * SLOTS + g + 1)
                for k in range(TILES):
                    if it == 0 and g == 0:
                        pe.wait_ge(drained, b * TILES + k + 1)
                    for c in range(QUAD):
                        chunk, o = it * BODY + g * QUAD + c, c * ROWS + k * P
                        for m, val in ((0, val1), (1, val2)):
                            ins = pe.matmul(acc[:, k, m * 2 * W:(m + 1) * 2 * W], split[:, g % SPLIT_RING, m, o:o + P],
                                            val[:, chunk, :], start=it == 0 and g == 0 and c == 0 and m == 0,
                                            stop=last_quad and c == QUAD - 1, skip_group_check=True)
                    if last_quad and k < TILES - 1:
                        ins.then_inc(tile_done, 1)
                ins.then_inc(used, 1)

            def add_h_parts():
                pe.wait_ge(h_parts, H_STEPS + 1)
                pe.matmul(h_psum, ones[:], h_part[:], start=True, stop=True).then_inc(h_added, 1)

            def body(b, it, ahead, first=False):
                for g in range(SLOTS):
                    n = g + TURN_RING
                    if n < SLOTS or ahead:
                        pe.wait_ge(split_done, (b * ITERS + it) * SLOTS + g + 1)
                        if n < SLOTS:
                            turn(b, it, n)
                        else:
                            turn(*ahead, n - SLOTS)
                    if first and g * QUAD % PART == 0:
                        pe.wait_ge((values_ready, rests_ready)[it], 2 * (g * QUAD // PART + 1))
                    add(b, it, g, it == ITERS - 1 and g == SLOTS - 1)

            for g in range(TURN_RING):
                turn(0, 0, g)
            pe.wait_ge(parts_ready, 3)
            pe.transpose(s_psum[:, 0:P], s_parts[:, 0:2, :], ident_b[:])
            pe.transpose(s_psum[0:NC, P:2 * P], s_parts[:, 2, :], ident_b[:]).then_inc(s_turned, 1)
            pe.wait_ge(pick_ready, 1)
            pe.wait_ge(s_t_ready, 2)
            for g in range(GROUPS):
                if g >= 2:
                    wait_s_row(pe, g - 1)
                for c in range(g * GC, (g + 1) * GC):
                    o = c % (2 * GC) * P
                    pe.matmul(row_psum[:, o:o + P], pick[:, c:c + 1].to_broadcast([P, P]), s_t[:, 0, :],
                              start=True, stop=False)
                    ins = pe.matmul(row_psum[:, o:o + P], pick[0:NC, c:c + 1].to_broadcast([NC, P]), s_t[0:NC, 1, :],
                                    start=False, stop=True)
                ins.then_inc(s_spread, 1)
            pe.wait_ge(wide_ready, 1)
            with pe.If(pe.value_load(wide_i[0:1, 0:1], min_val=0, max_val=1) == 0):
                wait_s_row(pe, GROUPS)
                body(0, 0, (0, 1), first=True)
                body(0, 1, (1, 0), first=True)
                add_h_parts()
                with pe.Fori(1, NB - 1) as b:
                    body(b, 0, (b, 1))
                    body(b, 1, (b + 1, 0))
                body(NB - 1, 0, (NB - 1, 1))
                body(NB - 1, 1, None)
            with pe.Else():
                wait_s_row(pe, GROUPS)
                add_h_parts()
                pe.wait_ge(h_sum_ready, 1)
                general_pe(pe)

        @block.vector
        def _(v):
            steps = [0]

            def link(ins):
                steps[0] += 1
                ins.then_inc(dve_seq, 1)
                v.wait_ge(dve_seq, steps[0])

            def take_s_row(g):
                dst, src = s_row_group(g)
                v.wait_ge(s_spread, g + 1)
                v.tensor_copy(dst, src).then_inc(s_row_ready["dve"], 1)

            def per_chunk(ap, n):
                return ap.unsqueeze(2).to_broadcast([P, ap.shape[1], n])

            v.memset(zero_w[:], 0.0).then_inc(consts_set, 1)
            v.memset(zero_v[:], 0.0).then_inc(consts_set, 1)
            v.memset(ones[:], 1.0).then_inc(consts_set, 1)
            v.memset(low[:], LOW).then_inc(consts_set, 1)
            v.wait_ge(ident_set, 2)
            v.tensor_tensor(pick[:], ident_b[:, 0:NC], ident_b[:, NC:2 * NC], ALU.add).then_inc(pick_ready, 1)
            for i in range(2):
                for n in ((0, 1), (2,))[i]:
                    v.wait_ge(x_in[n], 16)
                    link(v.tensor_reduce(mean[:, pieces[n]], h[:, pieces[n]], AX.X, ALU.add))
                link(v.tensor_scalar(mean[:, half[i]], mean[:, half[i]], 1.0 / D, None, ALU.mult))
                v.tensor_tensor(h[:, half[i]], h[:, half[i]], per_chunk(mean[:, half[i]], D),
                                ALU.subtract).then_inc(centred, 1)
            for i in range(2):
                v.wait_ge(squared, i + 1)
                link(v.tensor_reduce(var[:, half[i]], prod[:, half[i]], AX.X, ALU.add))
            v.tensor_scalar(var[:], var[:], 1.0 / D, EPS, ALU.mult, ALU.add).then_inc(var_ready, 1)
            v.wait_ge(a_in, 16)
            v.wait_ge(kept, 2)
            v.tensor_tensor(prod[:], h[:], a_b[:, 0:D].unsqueeze(1).to_broadcast([P, NC, D]),
                            ALU.mult).then_inc(prod_ready, 1)
            v.wait_ge(std_ready, 1)
            link(v.reciprocal(quo[:], std[:]))
            link(v.tensor_tensor(quo[:], quo[:], var[:], ALU.mult))
            link(v.tensor_tensor(quo[:], quo[:], std[:], ALU.add))
            link(v.tensor_scalar(quo[:], quo[:], 0.5, None, ALU.mult))
            v.reciprocal(rstd[:], quo[:]).then_inc(rstd_ready, 1)
            v.wait_ge(prod_ready, 1)
            link(v.tensor_reduce(s_raw[:], prod[:], AX.X, ALU.add))
            v.wait_ge(rstd_ready, 1)
            link(v.tensor_tensor(s[:], s_raw[:], rstd[:], ALU.mult))
            v.tensor_copy(s_parts[:, 0], s[:]).then_inc(parts_ready, 1)
            v.wait_ge(parts_ready, 1)
            link(v.tensor_tensor(s_left[:], s[:], s_parts[:, 0], ALU.subtract))
            v.tensor_copy(s_parts[:, 1], s_left[:]).then_inc(parts_ready, 1)
            v.wait_ge(parts_ready, 2)
            v.tensor_tensor(s_parts[:, 2], s_left[:], s_parts[:, 1], ALU.subtract).then_inc(parts_ready, 1)
            v.wait_ge(prod_t_ready, 2)
            link(v.tensor_reduce(t_raw[:], prod_t[:], AX.X, ALU.add))
            link(v.tensor_tensor(t[:], t_raw[:], rstd[:], ALU.mult))
            v.tensor_reduce(ext[:, 0:1], t[:], AX.X, ALU.max).then_inc(ext_ready, 1)
            link(v.tensor_scalar(neg_t[:], t[:], -1.0, None, ALU.mult))
            v.tensor_reduce(ext[:, 1:2], neg_t[:], AX.X, ALU.max).then_inc(ext_ready, 1)
            v.tensor_scalar(t_big[:], t[:], BIG, None, ALU.mult).then_inc(t_big_ready, 1)
            v.wait_ge(top_ready, 1)
            v.tensor_scalar(eb[:, 0:1], top[:, 0:1], -1.0, None, ALU.mult).then_inc(exp_bias, 1)
            v.tensor_scalar(eb[:, 1:2], top[:, 0:1], -LEAK, None, ALU.mult).then_inc(exp_bias, 1)
            v.wait_ge(table_in, 1)
            link(v.tensor_tensor(wide[:], top[:, 0:1], top[:, 1:2], ALU.add))
            v.tensor_scalar(wide_i[:], wide[:], SPAN, None, ALU.is_gt).then_inc(wide_ready, 1)
            v.wait_ge(exp_ready, 2)
            v.tensor_scalar(bexp_2[:], bexp[:], SCALE, None, ALU.mult).then_inc(exp_scaled, 1)
            v.tensor_scalar(dexp_2[:], dexp[:], SCALE, None, ALU.mult).then_inc(exp_scaled, 1)
            v.tensor_scalar(bexp[:], bexp[:], SCALE * LOW, None, ALU.mult).then_inc(exp_scaled, 1)
            v.tensor_scalar(dexp[:], dexp[:], SCALE * LOW, None, ALU.mult).then_inc(exp_scaled, 1)
            v.wait_ge(exp_scaled, 4)
            v.wait_ge(h_ready, 2)
            make_big(v, 0)

            def rest(i):
                for k, val in ((0, val1), (1, val2)):
                    v.wait_ge(near_ready[i], k + 1)
                    v.scalar_tensor_tensor(out=val[:, part[i], W:2 * W], in0=val[:, part[i], 0:W], scalar=-LOW,
                                           in1=big[:, i % 2, k], op0=ALU.mult, op1=ALU.add).then_inc(values_ready, 1)

            rest(0)
            take_s_row(5)
            take_s_row(6)

            def body(b, it, first=False, invert_at=None, finish_at=None, early=False, between=None):
                for g in range(SLOTS):
                    q, r = (b * ITERS + it) * SLOTS + g, g % SPLIT_RING
                    edge = turned[:, g % TURN_RING].bitcast(F16)
                    v.wait_ge(turn_done, q + 1)
                    v.wait_ge(side_done, q + 1)
                    if not first or g >= SPLIT_RING:
                        v.wait_ge(used, q - SPLIT_RING + 1)
                    v.tensor_tensor(split[:, r, 1], edge, side[:, g % SIDE_RING], ALU.is_gt).then_inc(neg_done, 1)
                    v.wait_ge(neg_done, q + 1)
                    v.tensor_tensor(split[:, r, 0], edge, split[:, r, 1].bitcast(I16), ALU.is_gt).then_inc(split_done, 1)
                    if between and g in between:
                        between[g]()
                    if g == invert_at:
                        invert(b - 1)
                    if g == finish_at:
                        if not early:
                            v.wait_ge(y_out, 16 * (b - 1))
                        finish(b - 1)

            def invert(b):
                v.wait_ge(combined, b + 1)
                v.tensor_scalar(lone[:], total[:, :, D], 0.0, None, ALU.is_equal).then_inc(inv_done, 1)
                v.wait_ge(inv_done, 3 * b + 1)
                v.scalar_tensor_tensor(out=den[:], in0=lone[:], scalar=float(N), in1=total[:, :, D], op0=ALU.mult,
                                       op1=ALU.add).then_inc(inv_done, 1)
                v.wait_ge(inv_done, 3 * b + 2)
                v.reciprocal(inv[:], den[:]).then_inc(inv_done, 1)

            def finish(b):
                v.wait_ge(att_done, b + 1)
                v.wait_ge(x_block_in, 16 * (b + 1))
                v.scalar_tensor_tensor(out=y[:], in0=att[:], scalar=0.0, in1=x_block[:],
                                       op0=ALU.max, op1=ALU.add).then_inc(y_done, 1)

            def row_arguments():
                link(v.tensor_scalar(xs[:], s[:], top[:, 0:1], None, ALU.add))
                link(v.scalar_tensor_tensor(out=xm[:], in0=xs[:], scalar=LEAK, in1=xs[:], op0=ALU.mult, op1=ALU.max))
                v.tensor_tensor(x1[:], xs[:], xm[:], ALU.subtract).then_inc(row_args, 1)
                v.scalar_tensor_tensor(out=x2[:], in0=xs[:], scalar=LEAK, in1=xm[:], op0=ALU.mult,
                                       op1=ALU.subtract).then_inc(row_args, 1)

            def row_factors():
                v.wait_ge(row_exp, 2)
                for k, e in ((0, e1), (2, e2)):
                    v.tensor_copy(coef[:, :, k], e[:]).then_inc(coef_ready, 1)
                    v.tensor_scalar(coef[:, :, k + 1], e[:], 1.0 / LOW, None, ALU.mult).then_inc(coef_ready, 1)

            def last_steps():
                rest(1)
                v.wait_ge(h_parts, H_STEPS + 1)

            v.wait_ge(wide_ready, 1)
            with v.If(v.value_load(wide_i[0:1, 0:1], min_val=0, max_val=1) == 0):
                body(0, 0, first=True, between={0: lambda: take_s_row(7), 1: last_steps})
                body(0, 1, between={1: row_arguments, 6: row_factors})
                body(1, 0)
                body(1, 1, invert_at=1, finish_at=3, early=True)
                with v.Fori(2, NB) as b:
                    body(b, 0)
                    body(b, 1, invert_at=1, finish_at=3)
                v.wait_ge(att_done, NB - 1)
                for k in range(TILES):
                    if k < TILES - 1:
                        v.wait_ge(tile_done, (NB - 1) * (TILES - 1) + k + 1)
                    else:
                        v.wait_ge(used, NB * ITERS * SLOTS)
                    last = v.tensor_tensor(sums[:, k], acc[:, k, 0:4 * W].rearrange("p (k w) -> p k w", w=W),
                                           coef[:, (NB - 1) * TILES + k, :].unsqueeze(2).to_broadcast([P, 4, W]),
                                           ALU.mult)
                link(last)
                link(v.tensor_tensor(comb[:], sums[:, :, 0:2], sums[:, :, 2:4], ALU.add))
                link(v.tensor_tensor(total[:], comb[:, :, 0], comb[:, :, 1], ALU.add))
                link(v.tensor_scalar(lone[:], total[:, :, D], 0.0, None, ALU.is_equal))
                v.scalar_tensor_tensor(out=den[:], in0=lone[:], scalar=float(N), in1=total[:, :, D], op0=ALU.mult,
                                       op1=ALU.add)
                link(v.tensor_tensor(fill[:], h_sum[:].unsqueeze(1).to_broadcast([P, TILES, D]),
                                     lone[:].unsqueeze(2).to_broadcast([P, TILES, D]), ALU.mult))
                v.reciprocal(inv[:], den[:])
                link(v.tensor_tensor(filled[:], total[:, :, 0:D], fill[:], ALU.add))
                link(v.tensor_tensor(att[:], filled[:], inv[:].unsqueeze(2).to_broadcast([P, TILES, D]), ALU.mult))
                v.wait_ge(x_block_in, 16 * NB)
                v.wait_ge(y_out, 16 * (NB - 1))
                v.scalar_tensor_tensor(out=y[:], in0=att[:], scalar=0.0, in1=x_block[:], op0=ALU.max,
                                       op1=ALU.add).then_inc(y_done, 1)
            with v.Else():
                take_s_row(7)
                last_steps()
                general_v(v)
    return nc


def kernel(**inputs):
    import numpy as _np
    import concourse.bacc as _bacc
    from concourse import mybir as _mybir
    from concourse.bass_utils import run_bass_kernel_spmd as _run

    nc = _bacc.Bacc("TRN2", target_bir_lowering=False, num_devices=1)
    arrays, args = {}, []
    for name in ("x", "adj", "L0_gnn_a"):
        v = _np.ascontiguousarray(inputs[name])
        arrays[f"in_{name}"] = v
        args.append(nc.dram_tensor(f"in_{name}", v.shape, _mybir.dt.from_np(v.dtype), kind="ExternalInput").ap())
    out = nc.dram_tensor("out", inputs["x"].shape, _mybir.dt.float32, kind="ExternalOutput").ap()
    gat_layer(nc, *args, out)
    r = _run(nc, [arrays], core_ids=[0])
    return r.results[0]["out"]
```
